# Optimizing a Trainium2 kernel written in Bass

```python
import numpy as np
import jax
import jax.numpy as jnp

def _softmax(x, axis=-1):
    return jax.nn.softmax(x, axis=axis)

def _gelu(x):
    return jax.nn.gelu(x, approximate=True)

def _silu(x):
    return jax.nn.silu(x)

def _sigmoid(x):
    return jax.nn.sigmoid(x)

def _layernorm(x, axis=-1, eps=1e-05):
    m = jnp.mean(x, axis=axis, keepdims=True)
    v = jnp.var(x, axis=axis, keepdims=True)
    return (x - m) / jnp.sqrt(v + eps)

def _scatter_add(tgt, idx, src, axis=0):
    return tgt.at[idx].add(src)

def _segment_sum(src, seg, n):
    return jax.ops.segment_sum(src, seg, n)
kernel_name = 'mk_sandwich_d1_jaxref_r4_c83c6a'

def setup_inputs(seed: int=0):
    np.random.seed(seed)
    _w = jnp.asarray

    def _L0_attn_setup():
        import jax, jax.numpy as jnp
        import numpy as np
        import math
        D_MODEL = 256
        D_STATE = 16
        D_INNER = 512
        DT_RANK = 64
        DT_MIN, DT_MAX = (0.001, 0.1)
        BATCH, SEQ_LEN = (4, 1024)
        key = jax.random.key(seed)
        k_x, k_wx, k_wdt, k_dt = jax.random.split(key, 4)
        x = jax.random.normal(k_x, (BATCH, SEQ_LEN, D_INNER), dtype=jnp.float32)
        A_log = jnp.log(jnp.tile(jnp.arange(1, D_STATE + 1, dtype=jnp.float32), (D_INNER, 1)))
        D_skip = jnp.ones((D_INNER,), dtype=jnp.float32)
        W_x = jax.random.normal(k_wx, (D_INNER, DT_RANK + 2 * D_STATE), dtype=jnp.float32) / math.sqrt(D_INNER)
        W_dt = jax.random.normal(k_wdt, (DT_RANK, D_INNER), dtype=jnp.float32) / math.sqrt(DT_RANK)
        dt_init = jnp.exp(jax.random.uniform(k_dt, (D_INNER,), dtype=jnp.float32) * (math.log(DT_MAX) - math.log(DT_MIN)) + math.log(DT_MIN))
        b_dt = dt_init + jnp.log(-jnp.expm1(-dt_init))
        return {'x': x, 'A_log': A_log, 'D_skip': D_skip, 'W_x': W_x, 'W_dt': W_dt, 'b_dt': b_dt}
    _L0_attn_in = _L0_attn_setup()

    def _L0_ffn_setup():
        import jax, jax.numpy as jnp
        import numpy as np
        from jax import lax
        DIM = 512
        E = 8
        K = 2
        RANK = 32
        CAP_FACTOR = 1.25

        def gelu(x):
            return jax.nn.gelu(x, approximate=False)

        def _moe_forward(x, gate_w, w1, b1, w2, b2, wd, wu, sw1, sb1, sw2, sb2, swd, swu):
            B, S, D = x.shape
            T = B * S
            cap = max(1, int(T * CAP_FACTOR / E))
            xt = x.reshape(T, D)
            logits = xt @ gate_w
            probs_full = jax.nn.softmax(logits, axis=-1)
            top_p, top_i = lax.top_k(probs_full, K)
            out = jnp.zeros_like(xt)
            for k in range(K):
                e = top_i[:, k]
                w = top_p[:, k]
                onehot = jax.nn.one_hot(e, E, dtype=jnp.int32)
                pos_all = jnp.cumsum(onehot, axis=0) - 1
                pos = jnp.take_along_axis(pos_all, e[:, None], axis=1)[:, 0]
                keep = pos < cap
                pos_c = jnp.where(keep, pos, cap)
                buf = jnp.zeros((E, cap, D), x.dtype).at[e, pos_c].set(xt * keep[:, None].astype(x.dtype), mode='drop')
                h = gelu(jnp.einsum('ecd,edf->ecf', buf, w1) + b1[:, None, :])
                y = jnp.einsum('ecf,efd->ecd', h, w2) + b2[:, None, :]
                a = jnp.einsum('ecr,erd->ecd', gelu(jnp.einsum('ecd,edr->ecr', buf, wd)), wu)
                y = y + a
                tok = y[e, jnp.minimum(pos_c, cap - 1)]
                out = out + tok * keep[:, None].astype(x.dtype) * w[:, None]
            sh = gelu(xt @ sw1 + sb1) @ sw2 + sb2
            sh = sh + gelu(xt @ swd) @ swu
            out = out + 0.2 * sh
            return out.reshape(B, S, D)
        key = jax.random.key(seed)
        ks = jax.random.split(key, 16)
        s = 0.02
        d, h = (DIM, 4 * DIM)
        inp = {'x': jax.random.normal(ks[0], (4, 512, d), dtype=jnp.float32), 'gate_w': jax.random.normal(ks[1], (d, E), dtype=jnp.float32) * s, 'w1': jax.random.normal(ks[2], (E, d, h), dtype=jnp.float32) * s, 'b1': jnp.zeros((E, h), dtype=jnp.float32), 'w2': jax.random.normal(ks[3], (E, h, d), dtype=jnp.float32) * s, 'b2': jnp.zeros((E, d), dtype=jnp.float32), 'wd': jax.random.normal(ks[4], (E, d, RANK), dtype=jnp.float32) * s, 'wu': jax.random.normal(ks[5], (E, RANK, d), dtype=jnp.float32) * s, 'sw1': jax.random.normal(ks[6], (d, h), dtype=jnp.float32) * s, 'sb1': jnp.zeros((h,), dtype=jnp.float32), 'sw2': jax.random.normal(ks[7], (h, d), dtype=jnp.float32) * s, 'sb2': jnp.zeros((d,), dtype=jnp.float32), 'swd': jax.random.normal(ks[8], (d, RANK), dtype=jnp.float32) * s, 'swu': jax.random.normal(ks[9], (RANK, d), dtype=jnp.float32) * s}
        return inp
    _L0_ffn_in = _L0_ffn_setup()
    _d = {'L0_attn_x': _L0_attn_in['x'], 'L0_attn_A_log': _L0_attn_in['A_log'], 'L0_attn_D_skip': _L0_attn_in['D_skip'], 'L0_attn_W_x': _L0_attn_in['W_x'], 'L0_attn_W_dt': _L0_attn_in['W_dt'], 'L0_attn_b_dt': _L0_attn_in['b_dt'], 'L0_ffn_gate_w': _L0_ffn_in['gate_w'], 'L0_ffn_w1': _L0_ffn_in['w1'], 'L0_ffn_b1': _L0_ffn_in['b1'], 'L0_ffn_w2': _L0_ffn_in['w2'], 'L0_ffn_b2': _L0_ffn_in['b2'], 'L0_ffn_wd': _L0_ffn_in['wd'], 'L0_ffn_wu': _L0_ffn_in['wu'], 'L0_ffn_sw1': _L0_ffn_in['sw1'], 'L0_ffn_sb1': _L0_ffn_in['sb1'], 'L0_ffn_sw2': _L0_ffn_in['sw2'], 'L0_ffn_sb2': _L0_ffn_in['sb2'], 'L0_ffn_swd': _L0_ffn_in['swd'], 'L0_ffn_swu': _L0_ffn_in['swu']}
    _x0 = _d['L0_attn_x']
    _d['L0_attn_x'] = jax.random.normal(jax.random.fold_in(jax.random.key(seed), 1), (1, 4096, 512), dtype=_x0.dtype)
    del _x0
    return _d

def reference(L0_attn_x, L0_attn_A_log, L0_attn_D_skip, L0_attn_W_x, L0_attn_W_dt, L0_attn_b_dt, L0_ffn_gate_w, L0_ffn_w1, L0_ffn_b1, L0_ffn_w2, L0_ffn_b2, L0_ffn_wd, L0_ffn_wu, L0_ffn_sw1, L0_ffn_sb1, L0_ffn_sw2, L0_ffn_sb2, L0_ffn_swd, L0_ffn_swu):

    def _L0_attn_ref(x, A_log, D_skip, W_x, W_dt, b_dt):
        import jax, jax.numpy as jnp
        import numpy as np
        import math
        D_MODEL = 256
        D_STATE = 16
        D_INNER = 512
        DT_RANK = 64
        DT_MIN, DT_MAX = (0.001, 0.1)
        BATCH, SEQ_LEN = (4, 1024)
        N = D_STATE
        xp = jnp.einsum('bld,de->ble', x, W_x)
        dt_low = xp[..., :DT_RANK]
        B_proj = xp[..., DT_RANK:DT_RANK + N]
        C_proj = xp[..., DT_RANK + N:]
        dt = jax.nn.softplus(jnp.einsum('blr,rd->bld', dt_low, W_dt) + b_dt)
        A = -jnp.exp(A_log)

        def step(h, inp):
            dt_t, Bp_t, C_t, x_t = inp
            dA = jnp.exp(dt_t[..., None] * A)
            h = dA * h + (dt_t * x_t)[..., None] * Bp_t[:, None, :]
            y = jnp.einsum('bdn,bn->bd', h, C_t)
            return (h, y)
        h0 = jnp.zeros((x.shape[0], D_INNER, N), dtype=x.dtype)
        xs = (jnp.swapaxes(dt, 0, 1), jnp.swapaxes(B_proj, 0, 1), jnp.swapaxes(C_proj, 0, 1), jnp.swapaxes(x, 0, 1))
        _, ys = jax.lax.scan(step, h0, xs)
        y = jnp.swapaxes(ys, 0, 1) + x * D_skip
        return y

    def _L0_ffn_ref(x, gate_w, w1, b1, w2, b2, wd, wu, sw1, sb1, sw2, sb2, swd, swu):
        import jax, jax.numpy as jnp
        import numpy as np
        from jax import lax
        DIM = 512
        E = 8
        K = 2
        RANK = 32
        CAP_FACTOR = 1.25

        def gelu(x):
            return jax.nn.gelu(x, approximate=False)

        def _moe_forward(x, gate_w, w1, b1, w2, b2, wd, wu, sw1, sb1, sw2, sb2, swd, swu):
            B, S, D = x.shape
            T = B * S
            cap = max(1, int(T * CAP_FACTOR / E))
            xt = x.reshape(T, D)
            logits = xt @ gate_w
            probs_full = jax.nn.softmax(logits, axis=-1)
            top_p, top_i = lax.top_k(probs_full, K)
            out = jnp.zeros_like(xt)
            for k in range(K):
                e = top_i[:, k]
                w = top_p[:, k]
                onehot = jax.nn.one_hot(e, E, dtype=jnp.int32)
                pos_all = jnp.cumsum(onehot, axis=0) - 1
                pos = jnp.take_along_axis(pos_all, e[:, None], axis=1)[:, 0]
                keep = pos < cap
                pos_c = jnp.where(keep, pos, cap)
                buf = jnp.zeros((E, cap, D), x.dtype).at[e, pos_c].set(xt * keep[:, None].astype(x.dtype), mode='drop')
                h = gelu(jnp.einsum('ecd,edf->ecf', buf, w1) + b1[:, None, :])
                y = jnp.einsum('ecf,efd->ecd', h, w2) + b2[:, None, :]
                a = jnp.einsum('ecr,erd->ecd', gelu(jnp.einsum('ecd,edr->ecr', buf, wd)), wu)
                y = y + a
                tok = y[e, jnp.minimum(pos_c, cap - 1)]
                out = out + tok * keep[:, None].astype(x.dtype) * w[:, None]
            sh = gelu(xt @ sw1 + sb1) @ sw2 + sb2
            sh = sh + gelu(xt @ swd) @ swu
            out = out + 0.2 * sh
            return out.reshape(B, S, D)
        return _moe_forward(x, gate_w, w1, b1, w2, b2, wd, wu, sw1, sb1, sw2, sb2, swd, swu)
    x = L0_attn_x
    x = x + _layernorm(_L0_attn_ref(_layernorm(x, axis=-1), L0_attn_A_log, L0_attn_D_skip, L0_attn_W_x, L0_attn_W_dt, L0_attn_b_dt), axis=-1)
    x = x + _layernorm(_L0_ffn_ref(_layernorm(x, axis=-1), L0_ffn_gate_w, L0_ffn_w1, L0_ffn_b1, L0_ffn_w2, L0_ffn_b2, L0_ffn_wd, L0_ffn_wu, L0_ffn_sw1, L0_ffn_sb1, L0_ffn_sw2, L0_ffn_sb2, L0_ffn_swd, L0_ffn_swu), axis=-1)
    return x

_drawn_inputs = setup_inputs


def setup_inputs(seed=0):
    import zlib

    import numpy as np

    out = dict(_drawn_inputs(seed))
    spreads = {'L0_attn_D_skip': (1.0, 0.2),
     'L0_ffn_b1': (0.0, 0.1),
     'L0_ffn_b2': (0.0, 0.1),
     'L0_ffn_sb1': (0.0, 0.1),
     'L0_ffn_sb2': (0.0, 0.1)}
    factors = {}
    for name, (base, spread) in spreads.items():
        noise = np.random.default_rng([zlib.crc32(name.encode()), seed]).standard_normal(out[name].shape)
        drawn = base * np.exp(spread * noise) if base else spread * noise
        out[name] = jnp.asarray(drawn.astype(out[name].dtype))
    for name, factor in factors.items():
        out[name] = (out[name] * factor).astype(out[name].dtype)
    return out
```

```python
from contextlib import ExitStack

import concourse.bass as bass
from concourse import mybir

F32 = mybir.dt.float32
F32R = mybir.dt.float32r
I32 = mybir.dt.int32
ALU = mybir.AluOpType
ACT = mybir.ActivationFunctionType
AXX = mybir.AxisListType.X

P = 128
T, D = 4096, 512
NS, RANK = 16, 64
DT = D // P
CH = 512
CT = CH // P
NCH = T // CH
NT = T // P
E, K = 8, 2
CAP = int(T * 1.25 / E)
SLOTS = K * CAP
FF, LR = 4 * D, 32
FC = FF // P
EPS = 1e-5


def after(eng, sem, value):
    if isinstance(value, int) and value <= 0:
        return
    eng.wait_ge(sem, value)


def pass_gate(eng, sem, value, gate):
    after(eng, sem, value)
    eng.sem_inc(gate, 1)


def in_pairs(eng, body, first, last):
    body(first, 0)
    body(first, 1)
    with eng.Fori(first + 1, last) as i:
        body(i, 0)
        body(i, 1)


def before(i, q):
    return (i, 0) if q else (i - 1, 1)


def prepare(nc, sem, const, x, A_log, D_skip, W_x, W_dt, b_dt, dt_d, dtx_d, bc_d, skip_d):
    ident, A_neg, eps = const["ident"], const["A_neg"], const["eps"]
    NX = RANK + 2 * NS
    with ExitStack() as ctx:
        def sb(name, shape, dt=F32):
            return ctx.enter_context(nc.sbuf_tensor(name, shape, dt))

        def two(name, shape):
            return [sb(f"{name}{q}", shape) for q in range(2)]

        wx = sb("wx", [P, DT, NX])
        wdt = sb("wdt", [RANK, D])
        bdt = sb("bdt", [P, DT])
        alog = sb("alog", [P, DT, NS])
        dbc = sb("dbc", [P, D])
        xin, xn, xnT = two("xin", [P, CT, D]), two("xn", [P, CT, D]), two("xnT", [P, DT, CH])
        st, mv = two("st", [P, CT, 6]), two("mv", [P, CT, 2])
        sd, rstd, nmr = two("sd", [P, CT]), two("rstd", [P, CT]), two("nmr", [P, CT])
        xpT = two("xpT", [NX, CH])
        au = two("au", [P, DT, CH])
        w1 = two("w1", [P, DT, CH])
        lg = two("lg", [P, DT, CH])
        dd = two("dd", [P, DT, CH])
        rz = two("rz", [P, DT, CH])
        dx = two("dx", [P, DT, CH])
        sk = two("sk", [P, CT, D])
        psT = [ctx.enter_context(nc.psum_tensor(f"a_psT{q}", [P, CH], F32)) for q in range(2)]
        psX = ctx.enter_context(nc.psum_tensor("a_psX", [P, CH], F32))
        psZ = ctx.enter_context(nc.psum_tensor("a_psZ", [P, DT, CH], F32))

        s_w, s_alog = sem("a_weights"), sem("a_alog_in")
        s_ident0, s_ident, s_eps = sem("a_ident_zero"), sem("a_ident"), sem("a_eps")
        s_ea, s_A = sem("a_expA"), sem("a_A")
        s_xin = [sem(f"a_x_in{q}") for q in range(2)]
        s_st, s_mv, s_sd, s_rs, s_nm = (sem(f"a_{n}") for n in ("stats", "meanvar", "std", "rstd", "nmr"))
        s_xn, s_xT, s_xnT, s_xp, s_xpT, s_z = (
            sem(f"a_{n}") for n in ("normed", "transposed", "xnT", "xp", "xpT", "z"))
        s_az, s_rz, s_u, s_w1, s_lg, s_dd, s_rd, s_lu, s_lp, s_dt, s_dx, s_sk = (
            sem(f"a_{n}") for n in ("absz", "reluz", "u", "w1", "ln", "d", "rd", "lnu", "log1p", "dt", "dtx", "skip"))
        g_sp, g_pool, g_dve = (sem(f"a_gate_{n}") for n in ("sp", "pool", "dve"))
        s_out = [sem(f"a_stored{q}") for q in range(2)]
        STORES = 5 * 16
        block = ctx.enter_context(nc.Block("prepare"))

        @block.sync
        def _(sp):
            def load(i, q):
                c = i * 2 + q
                pass_gate(sp, s_xn, (c - 1) * CT, g_sp)
                sp.dma_start(xin[q][:, :, :], x[bass.ds(c * CH, CH), :].rearrange("(t p) d -> p t d", p=P))\
                    .then_inc(s_xin[q], 16)

            def store(i, q):
                c = i * 2 + q
                cols = bass.ds(c * CH, CH)
                pass_gate(sp, s_xpT, c + 1, g_sp)
                sp.dma_start(bc_d[:, cols], xpT[q][RANK:NX, :]).then_inc(s_out[q], 16)
                pass_gate(sp, s_sk, (c + 1) * CT, g_sp)
                sp.dma_start(skip_d[bass.ds(c * CH, CH), :].rearrange("(t p) d -> p t d", p=P), sk[q][:, :, :])\
                    .then_inc(s_out[q], 16)
                pass_gate(sp, s_dt, c + 1, g_sp)
                sp.dma_start(dt_d[:, :, cols].rearrange("a p t -> p a t"), rz[q][:, :, :]).then_inc(s_out[q], 16)
                pass_gate(sp, s_dx, c + 1, g_sp)
                for h in range(2):
                    sp.dma_start(dtx_d[2 * h:2 * h + 2, :, cols].rearrange("a p t -> p a t"),
                                 dx[q][:, 2 * h:2 * h + 2, :]).then_inc(s_out[q], 16)

            def body(i, q):
                load(i, q)
                if not (isinstance(i, int) and i == 0 and q == 0):
                    store(*before(i, q))

            in_pairs(sp, body, 0, NCH // 2)
            store(NCH // 2 - 1, 1)
            for q in range(2):
                sp.wait_ge(s_out[q], STORES * NCH // 2)

        @block.gpsimd
        def _(pool):
            nc.gpsimd.memset(ident[:, :], 0.0).then_inc(s_ident0, 1)
            nc.gpsimd.memset(eps[:, :], EPS).then_inc(s_eps, 1)
            pool.wait_ge(s_ident0, 1)
            nc.gpsimd.affine_select(out=ident[:, :], in_=ident[:, :], compare_op=ALU.not_equal, fill=1.0,
                                    base=0, pattern=[[-1, P]], channel_multiplier=1).then_inc(s_ident, 1)
            pool.wait_ge(s_w, 64)

            def skip(i, q):
                c = i * 2 + q
                pool.wait_ge(s_xn, (c + 1) * CT)
                after(pool, s_out[q], i * STORES)
                for t in range(CT):
                    nc.gpsimd.tensor_tensor(sk[q][:, t, :], xn[q][:, t, :], dbc[:, :], ALU.mult).then_inc(s_sk, 1)

            def log1p(i, q):
                c = i * 2 + q
                pass_gate(pool, s_w1, c + 1, g_pool)
                nc.gpsimd.tensor_scalar(dd[q][:, :, :], w1[q][:, :, :], -1.0, 1.0, ALU.add, ALU.mult).then_inc(s_dd, 1)
                pool.wait_ge(s_lg, c + 1)
                nc.gpsimd.tensor_tensor(lg[q][:, :, :], lg[q][:, :, :], au[q][:, :, :], ALU.mult).then_inc(s_lu, 1)
                pool.wait_ge(s_rd, c + 1)
                pool.wait_ge(s_lu, c + 1)
                nc.gpsimd.tensor_tensor(lg[q][:, :, :], lg[q][:, :, :], dd[q][:, :, :], ALU.mult).then_inc(s_lp, 1)

            def body(i, q):
                if not (isinstance(i, int) and i == 0 and q == 0):
                    log1p(*before(i, q))
                skip(i, q)

            in_pairs(pool, body, 0, NCH // 2)
            log1p(NCH // 2 - 1, 1)

        @block.scalar
        def _(act):
            with nc.allow_non_contiguous_dma(reason="512 biases"):
                act.dma_start(bdt[:, :], b_dt.rearrange("(t p) -> p t", p=P)).then_inc(s_w, 16)
            act.dma_start(wx[:, :, :], W_x.rearrange("(t p) n -> p t n", p=P)).then_inc(s_w, 16)
            act.dma_start(wdt[:, :], W_dt).then_inc(s_w, 16)
            act.dma_start(dbc[:, :], D_skip.partition_broadcast(P)).then_inc(s_w, 16)
            act.dma_start(alog[:, :, :], A_log.rearrange("(t p) n -> p t n", p=P)).then_inc(s_alog, 16)
            act.wait_ge(s_alog, 16)
            nc.scalar.activation(A_neg[:, :, :], alog[:, :, :], ACT.Exp).then_inc(s_ea, 1)
            act.wait_ge(s_eps, 1)
            act.wait_ge(s_w, 64)

            def norm(i, q):
                c = i * 2 + q
                act.wait_ge(s_mv, (c + 1) * CT)
                nc.scalar.activation(sd[q][:, :], mv[q][:, :, 1], ACT.Sqrt, bias=eps[:, :]).then_inc(s_sd, 1)
                act.wait_ge(s_nm, c + 1)
                after(act, s_sk, (c - 1) * CT)
                after(act, s_xT, (c - 1) * DT)
                for t in range(CT):
                    nc.scalar.activation(xn[q][:, t, :], xin[q][:, t, :], ACT.Identity, bias=nmr[q][:, t:t + 1],
                                         scale=rstd[q][:, t:t + 1]).then_inc(s_xn, 1)

            def project(i, q):
                c = i * 2 + q
                act.wait_ge(s_xp, c + 1)
                after(act, s_z, c - 1)
                after(act, s_out[q], i * STORES)
                nc.scalar.copy(xpT[q][:, :], psX[0:NX, :]).then_inc(s_xpT, 1)

            def soft(i, q):
                c = i * 2 + q
                act.wait_ge(s_rz, (c + 1) * DT)
                after(act, s_lu, c - 1)
                nc.scalar.activation(au[q][:, :, :], rz[q][:, :, :], ACT.Abs).then_inc(s_az, 1)
                act.wait_ge(s_az, c + 1)
                nc.scalar.activation(au[q][:, :, :], au[q][:, :, :], ACT.Exp, scale=-1.0).then_inc(s_u, 1)
                act.wait_ge(s_w1, c + 1)
                after(act, s_dt, c - 1)
                nc.scalar.activation(lg[q][:, :, :], w1[q][:, :, :], ACT.Ln).then_inc(s_lg, 1)

            def body(i, q):
                norm(i, q)
                if not (isinstance(i, int) and i == 0 and q == 0):
                    soft(*before(i, q))
                project(i, q)

            in_pairs(act, body, 0, NCH // 2)
            soft(NCH // 2 - 1, 1)

        @block.vector
        def _(dve):
            dve.wait_ge(s_ea, 1)
            nc.vector.tensor_scalar(A_neg[:, :, :], A_neg[:, :, :], -1.0, None, ALU.mult).then_inc(s_A, 1)
            dve.wait_ge(s_w, 64)

            def stats(i, q):
                c = i * 2 + q
                dve.wait_ge(s_xin[q], (i + 1) * 16)
                for t in range(CT):
                    nc.vector.bn_stats(st[q][:, t, :], xin[q][:, t, :]).then_inc(s_st, 1)
                after(dve, s_sd, c - 1)
                for t in range(CT):
                    pass_gate(dve, s_st, c * CT + t + 1, g_dve)
                    nc.vector.bn_aggr(mv[q][:, t, :], st[q][:, t, :]).then_inc(s_mv, 1)

            def scale(i, q):
                c = i * 2 + q
                dve.wait_ge(s_sd, c + 1)
                after(dve, s_xn, (c - 1) * CT)
                nc.vector.reciprocal(rstd[q][:, :], sd[q][:, :]).then_inc(s_rs, 1)
                dve.wait_ge(s_rs, c + 1)
                dve.wait_ge(s_mv, (c + 1) * CT)
                nc.vector.scalar_tensor_tensor(nmr[q][:, :], mv[q][:, :, 0], -1.0, rstd[q][:, :], ALU.mult, ALU.mult)\
                    .then_inc(s_nm, 1)

            def evacuate(i, q):
                c = i * 2 + q
                after(dve, s_xp, c - 1)
                for t in range(DT):
                    dve.wait_ge(s_xT, c * DT + t + 1)
                    nc.vector.tensor_copy(xnT[q][:, t, :], psT[t % 2][:, :]).then_inc(s_xnT, 1)

            def soft_a(i, q):
                c = i * 2 + q
                dve.wait_ge(s_z, c + 1)
                after(dve, s_out[q], i * STORES)
                for t in range(DT):
                    nc.vector.tensor_scalar(rz[q][:, t, :], psZ[:, t, :], bdt[:, t:t + 1], None, ALU.add)\
                        .then_inc(s_rz, 1)

            def soft_b(i, q):
                c = i * 2 + q
                dve.wait_ge(s_u, c + 1)
                after(dve, s_lg, c - 1)
                after(dve, s_dd, c - 1)
                nc.vector.tensor_scalar(w1[q][:, :, :], au[q][:, :, :], 1.0, 1.0 + 2.0 ** -23, ALU.add, ALU.max)\
                    .then_inc(s_w1, 1)

            def soft_c(i, q):
                c = i * 2 + q
                dve.wait_ge(s_dd, c + 1)
                nc.vector.reciprocal(dd[q][:, :, :], dd[q][:, :, :]).then_inc(s_rd, 1)

            def soft_d(i, q):
                c = i * 2 + q
                dve.wait_ge(s_lp, c + 1)
                nc.vector.scalar_tensor_tensor(rz[q][:, :, :], rz[q][:, :, :], 0.0, lg[q][:, :, :], ALU.max, ALU.add)\
                    .then_inc(s_dt, 1)
                dve.wait_ge(s_dt, c + 1)
                after(dve, s_out[q], i * STORES)
                nc.vector.tensor_tensor(dx[q][:, :, :], rz[q][:, :, :], xnT[q][:, :, :], ALU.mult).then_inc(s_dx, 1)

            def body(i, q):
                back = not (isinstance(i, int) and i == 0 and q == 0)
                prev = before(i, q)
                stats(i, q)
                scale(i, q)
                if back:
                    soft_a(*prev)
                evacuate(i, q)
                if back:
                    soft_b(*prev)
                    soft_c(*prev)
                    soft_d(*prev)

            in_pairs(dve, body, 0, NCH // 2)
            tail = (NCH // 2 - 1, 1)
            soft_a(*tail)
            soft_b(*tail)
            soft_c(*tail)
            soft_d(*tail)

        @block.tensor
        def _(pe):
            pe.wait_ge(s_ident, 1)
            pe.wait_ge(s_w, 64)

            def body(i, q):
                c = i * 2 + q
                pe.wait_ge(s_xn, (c + 1) * CT)
                for d in range(DT):
                    after(pe, s_xnT, c * DT + d - 1)
                    for t in range(CT):
                        last = nc.tensor.transpose(psT[d % 2][:, t * P:(t + 1) * P],
                                                   xn[q][:, t, d * P:(d + 1) * P], ident[:, :])
                    last.then_inc(s_xT, 1)
                after(pe, s_xpT, c)
                for d in range(DT):
                    pe.wait_ge(s_xnT, c * DT + d + 1)
                    last = nc.tensor.matmul(psX[0:NX, :], wx[:, d, :], xnT[q][:, d, :],
                                            start=(d == 0), stop=(d == DT - 1))
                last.then_inc(s_xp, 1)
                pe.wait_ge(s_xpT, c + 1)
                after(pe, s_rz, c * DT)
                for d in range(DT):
                    last = nc.tensor.matmul(psZ[:, d, :], wdt[:, d * P:(d + 1) * P], xpT[q][0:RANK, :],
                                            start=True, stop=True)
                last.then_inc(s_z, 1)

            in_pairs(pe, body, 0, NCH // 2)


def scan(nc, sem, const, x, dt_d, dtx_d, bc_d, skip_d, x1_d):
    ident, A_neg, eps, mv1 = const["ident"], const["A_neg"], const["eps"], const["mv_x1"]
    NU = NS * DT
    NU_, NH_, NP_ = 3, 6, 6
    with ExitStack() as ctx:
        def sb(name, shape, dt=F32):
            return ctx.enter_context(nc.sbuf_tensor(name, shape, dt))

        def two(name, shape):
            return [sb(f"{name}{q}", shape) for q in range(2)]

        dts, dtx = two("dts", [P, DT, CH]), two("dtxs", [P, DT, CH])
        Bs = two("Bs", [NS, CH])
        Cb = two("Cb", [P, NS, CH])
        skp, xr = two("skp", [P, CT, D]), two("xr", [P, CT, D])
        u = [sb(f"u{k}", [P, CH]) for k in range(NU_)]
        h = [sb(f"h{k}", [P, CH]) for k in range(NH_)]
        pr = [sb(f"pr{k}", [P, CH]) for k in range(NP_)]
        carry = sb("carry", [P, NU])
        sel = sb("sel", [NS, NS, P])
        ys = sb("ys", [P, CT, D])
        yo = two("yo", [P, CT, D])
        st, mv = sb("b_st", [P, CT, 6]), sb("b_mv", [P, CT, 2])
        st2, mv2 = sb("b_st2", [P, CT, 6]), sb("b_mv2", [P, CT, 2])
        sd, rstd, nmr = sb("b_sd", [P, CT]), sb("b_rstd", [P, CT]), sb("b_nmr", [P, CT])
        psA = [ctx.enter_context(nc.psum_tensor(f"b_psA{q}", [P, CH], F32)) for q in range(2)]
        psB = [ctx.enter_context(nc.psum_tensor(f"b_psB{q}", [P, CH], F32)) for q in range(2)]
        psY = [ctx.enter_context(nc.psum_tensor(f"b_psY{t}", [P, D], F32)) for t in range(CT)]

        s_ld = [sem(f"b_loaded{q}") for q in range(2)]
        s_pl = [sem(f"b_post_loaded{q}") for q in range(2)]
        s_sel0, s_sel, s_c0 = sem("b_sel_zero"), sem("b_sel"), sem("b_carry_zero")
        s_dA, s_bb, s_u, s_h, s_ca, s_p, s_y = (
            sem(f"b_{n}") for n in ("dA", "B_spread", "u", "h", "carry", "hC", "y_added"))
        s_ys, s_st, s_mv, s_sd, s_rs, s_nm, s_yn, s_x1, s_st2, s_mv2, s_mv1 = (
            sem(f"b_{n}") for n in ("y_out", "stats", "meanvar", "std", "rstd", "nmr", "normed", "x1", "stats2", "meanvar2", "meanvar_x1"))
        g_sp, g_dve = sem("b_gate_sp"), sem("b_gate_dve")
        s_out = [sem(f"b_stored{q}") for q in range(2)]
        block = ctx.enter_context(nc.Block("scan"))

        @block.sync
        def _(sp):
            def load(i, q):
                c = i * 2 + q
                cols = bass.ds(c * CH, CH)
                pass_gate(sp, s_p, (c - 1) * NU, g_sp)
                sp.dma_start(dts[q][:, :, :], dt_d[:, :, cols].rearrange("a p t -> p a t")).then_inc(s_ld[q], 16)
                sp.dma_start(Bs[q][:, :], bc_d[0:NS, cols]).then_inc(s_ld[q], 16)
                sp.dma_start(dtx[q][:, :, :], dtx_d[:, :, cols].rearrange("a p t -> p a t")).then_inc(s_ld[q], 16)
                sp.dma_start(Cb[q][:, :, :], bc_d[NS:2 * NS, cols].partition_broadcast(P)).then_inc(s_ld[q], 16)
                pass_gate(sp, s_x1, (c - 1) * CT, g_sp)
                rows = bass.ds(c * CH, CH)
                sp.dma_start(skp[q][:, :, :], skip_d[rows, :].rearrange("(t p) d -> p t d", p=P))\
                    .then_inc(s_pl[q], 16)
                sp.dma_start(xr[q][:, :, :], x[rows, :].rearrange("(t p) d -> p t d", p=P)).then_inc(s_pl[q], 16)

            def store(i, q):
                c = i * 2 + q
                pass_gate(sp, s_x1, (c + 1) * CT, g_sp)
                sp.dma_start(x1_d[bass.ds(c * CH, CH), :].rearrange("(t p) d -> p t d", p=P), yo[q][:, :, :])\
                    .then_inc(s_out[q], 16)

            def body(i, q):
                load(i, q)
                if not (isinstance(i, int) and i == 0):
                    store(i - 1, q)

            in_pairs(sp, body, 0, NCH // 2)
            store(NCH // 2 - 1, 0)
            store(NCH // 2 - 1, 1)
            for q in range(2):
                sp.wait_ge(s_out[q], 16 * NCH // 2)

        @block.scalar
        def _(act):
            def decay(c, q, k):
                n, d = k // DT, k % DT
                after(act, s_h, c * NU + k - 1)
                nc.scalar.activation(psA[k % 2][:, :], dts[q][:, d, :], ACT.Exp,
                                     scale=A_neg[:, d, n:n + 1]).then_inc(s_dA, 1)

            def keep(c, k):
                act.wait_ge(s_h, c * NU + k + 1)
                nc.scalar.copy(carry[:, k:k + 1], h[(k % NH_)][:, CH - 1:CH]).then_inc(s_ca, 1)

            def std(c):
                act.wait_ge(s_mv, (c + 1) * CT)
                nc.scalar.activation(sd[:, :], mv[:, :, 1], ACT.Sqrt, bias=eps[:, :]).then_inc(s_sd, 1)

            def norm(c, q):
                act.wait_ge(s_nm, c + 1)
                after(act, s_out[q], (c - q) * 8)
                for t in range(CT):
                    nc.scalar.activation(yo[q][:, t, :], ys[:, t, :], ACT.Identity, bias=nmr[:, t:t + 1],
                                         scale=rstd[:, t:t + 1]).then_inc(s_yn, 1)

            act.wait_ge(s_c0, 1)

            def body(i, q):
                c = i * 2 + q
                post = not (isinstance(i, int) and i == 0 and q == 0)
                act.wait_ge(s_ld[q], (i + 1) * 64)
                decay(c, q, 0)
                decay(c, q, 1)
                for k in range(NU):
                    keep(c, k)
                    if k + 2 < NU:
                        decay(c, q, k + 2)
                    if post and k == 16:
                        std(c - 1)
                    if post and k == 22:
                        norm(c - 1, 1 - q)

            in_pairs(act, body, 0, NCH // 2)
            std(NCH - 1)
            norm(NCH - 1, 1)

        @block.vector
        def _(dve):
            nc.vector.memset(carry[:, :], 0.0).then_inc(s_c0, 1)

            def drive(c, q, k):
                n, d = k // DT, k % DT
                dve.wait_ge(s_bb, c * NS + n + 1)
                after(dve, s_h, c * NU + k - NU_ + 1)
                nc.vector.tensor_tensor(u[k % NU_][:, :], dtx[q][:, d, :], psB[n % 2][:, :], ALU.mult).then_inc(s_u, 1)

            def recur(c, k):
                g = c * NU + k
                dve.wait_ge(s_dA, g + 1)
                dve.wait_ge(s_u, g + 1)
                if k >= NH_:
                    dve.wait_ge(s_p, g - NH_ + 1)
                    dve.wait_ge(s_ca, g - NH_ + 1)
                else:
                    after(dve, s_p, c * NU)
                    after(dve, s_ca, c * NU)
                nc.vector.tensor_tensor_scan(h[k % NH_][:, :], psA[k % 2][:, :], u[k % NU_][:, :],
                                             carry[:, k:k + 1], ALU.mult, ALU.add).then_inc(s_h, 1)

            def take(c, q):
                dve.wait_ge(s_pl[q], (c - q) * 16 + 32)
                dve.wait_ge(s_y, (c + 1) * NU)
                after(dve, s_yn, c * CT)
                for t in range(CT):
                    nc.vector.tensor_tensor(ys[:, t, :], psY[t][:, :], skp[q][:, t, :], ALU.add).then_inc(s_ys, 1)

            def stats(c):
                dve.wait_ge(s_ys, (c + 1) * CT)
                for t in range(CT):
                    nc.vector.bn_stats(st[:, t, :], ys[:, t, :]).then_inc(s_st, 1)

            def aggregate(c):
                after(dve, s_sd, c)
                pass_gate(dve, s_st, (c + 1) * CT, g_dve)
                for t in range(CT):
                    nc.vector.bn_aggr(mv[:, t, :], st[:, t, :]).then_inc(s_mv, 1)

            def scale(c):
                dve.wait_ge(s_sd, c + 1)
                after(dve, s_yn, c * CT)
                nc.vector.reciprocal(rstd[:, :], sd[:, :]).then_inc(s_rs, 1)
                dve.wait_ge(s_rs, c + 1)
                nc.vector.scalar_tensor_tensor(nmr[:, :], mv[:, :, 0], -1.0, rstd[:, :], ALU.mult, ALU.mult)\
                    .then_inc(s_nm, 1)

            def residual(c, q):
                dve.wait_ge(s_yn, (c + 1) * CT)
                for t in range(CT):
                    nc.vector.tensor_tensor(yo[q][:, t, :], yo[q][:, t, :], xr[q][:, t, :], ALU.add).then_inc(s_x1, 1)

            def stats_x1(c, q):
                dve.wait_ge(s_x1, (c + 1) * CT)
                for t in range(CT):
                    nc.vector.bn_stats(st2[:, t, :], yo[q][:, t, :]).then_inc(s_st2, 1)

            def aggregate_x1(c):
                pass_gate(dve, s_st2, (c + 1) * CT, g_dve)
                for t in range(CT):
                    nc.vector.bn_aggr(mv2[:, t, :], st2[:, t, :]).then_inc(s_mv2, 1)
                dve.wait_ge(s_mv2, (c + 1) * CT)
                nc.vector.tensor_copy(mv1[:, bass.ds(c * CT, CT), :], mv2[:, :, :]).then_inc(s_mv1, 1)

            def body(i, q):
                c = i * 2 + q
                post = not (isinstance(i, int) and i == 0 and q == 0)
                dve.wait_ge(s_ld[q], (i + 1) * 64)
                drive(c, q, 0)
                for k in range(NU):
                    if k + 1 < NU:
                        drive(c, q, k + 1)
                    recur(c, k)
                    if post and k == 2:
                        take(c - 1, 1 - q)
                    if post and k == 8:
                        stats(c - 1)
                    if post and k == 12:
                        aggregate(c - 1)
                    if post and k == 20:
                        scale(c - 1)
                    if post and k == 30:
                        residual(c - 1, 1 - q)
                    if post and k == 36:
                        stats_x1(c - 1, 1 - q)
                    if post and k == 42:
                        aggregate_x1(c - 1)

            in_pairs(dve, body, 0, NCH // 2)
            take(NCH - 1, 1)
            stats(NCH - 1)
            aggregate(NCH - 1)
            scale(NCH - 1)
            residual(NCH - 1, 1)
            stats_x1(NCH - 1, 1)
            aggregate_x1(NCH - 1)

        @block.gpsimd
        def _(pool):
            nc.gpsimd.memset(sel[:, :, :], 0.0).then_inc(s_sel0, 1)
            pool.wait_ge(s_sel0, 1)
            nc.gpsimd.affine_select(out=sel[:, :, :], in_=sel[:, :, :], compare_op=ALU.not_equal, fill=1.0,
                                    base=0, pattern=[[-1, NS], [0, P]], channel_multiplier=1).then_inc(s_sel, 1)

            def body(i, q):
                c = i * 2 + q
                pool.wait_ge(s_ld[q], (i + 1) * 64)
                for k in range(NU):
                    g = c * NU + k
                    pool.wait_ge(s_h, g + 1)
                    if k >= NP_:
                        pool.wait_ge(s_y, g - NP_ + 1)
                    else:
                        after(pool, s_y, c * NU)
                    nc.gpsimd.tensor_tensor(pr[k % NP_][:, :], h[k % NH_][:, :], Cb[q][:, k // DT, :], ALU.mult)\
                        .then_inc(s_p, 1)

            in_pairs(pool, body, 0, NCH // 2)

        @block.tensor
        def _(pe):
            pe.wait_ge(s_sel, 1)

            def spread(c, q, n):
                if n >= 2:
                    pe.wait_ge(s_u, c * NU + (n - 1) * DT)
                else:
                    after(pe, s_u, c * NU)
                nc.tensor.matmul(psB[n % 2][:, :], sel[:, n, :], Bs[q][:, :], start=True, stop=True).then_inc(s_bb, 1)

            def body(i, q):
                c = i * 2 + q
                pe.wait_ge(s_ld[q], (i + 1) * 64)
                spread(c, q, 0)
                spread(c, q, 1)
                for k in range(NU):
                    n, d = k // DT, k % DT
                    if k == 0:
                        after(pe, s_ys, c * CT)
                    pe.wait_ge(s_p, c * NU + k + 1)
                    for t in range(CT):
                        last = nc.tensor.matmul(psY[t][:, d * P:(d + 1) * P], pr[k % NP_][:, t * P:(t + 1) * P],
                                                ident[:, :], start=(k == 0), stop=(k == NU - 1),
                                                skip_group_check=True)
                    last.then_inc(s_y, 1)
                    if d == DT - 1 and n + 2 < NS:
                        spread(c, q, n + 2)

            in_pairs(pe, body, 0, NCH // 2)


J = FC + 1
BT = 4
SB = T // (BT * P)
ST = SLOTS // P
EB = ((0, 2), (2, 4), (6, 4))
PIECES = 4 + 2 * FC
RING = 4
FRONT = (2, 6, 10, 14)
PICKED = 4 + 6 * K
LEAD = 3


def experts(nc, sem, const, w, x1_d, xt_d, sh_d, y_d, idx_d):
    ident, eps, mv1 = const["ident"], const["eps"], const["mv_x1"]
    wgt, row_g = const["wgt"], const["row_g"]
    with ExitStack() as ctx:
        def sb(name, shape, dt=F32, where=ctx):
            return where.enter_context(nc.sbuf_tensor(name, shape, dt))

        W1h, W1l = sb("W1h", [P, FC, DT, P], F32R), sb("W1l", [P, FC, DT, P], F32R)
        W2h, W2l = sb("W2h", [P, FC, D], F32R), sb("W2l", [P, FC, D], F32R)
        L1h, L1l = sb("L1h", [P, DT, P], F32R), sb("L1l", [P, DT, P], F32R)
        L2h, L2l = sb("L2h", [LR, D], F32R), sb("L2l", [LR, D], F32R)
        X = [(sb(f"X{n}h", [P, DT, r], F32R), sb(f"X{n}l", [P, DT, r], F32R)) for n, r in (("a", 512), ("b", 512))]
        h32 = sb("h32", [P, 512])
        hh = [sb(f"hh{q}", [P, 512], F32R) for q in range(2)]
        hl = [sb(f"hl{q}", [P, 512], F32R) for q in range(2)]
        raw = [sb(f"raw{q}", [P, 512]) for q in range(RING)]
        xrow = [sb(f"xrow{q}", [P, D]) for q in range(2)]
        yst = [sb(f"yst{q}", [P, D]) for q in range(2)]
        b2bc = sb("b2bc", [P, D])
        lg = sb("lg", [P, NT, E])
        b1T = sb("b1T", [P, (E + 1) * FC])
        b1e = sb("b1e", [P, FC])
        graw = sb("graw", [P, DT, E])
        rs1, nm1 = sb("rs1", [P, NT]), sb("nm1", [P, NT])
        idx = sb("idx", [P, ST], I32)
        rt = ExitStack()
        OH = sb("OH", [P, K, NT, E], F32, rt)
        RA = sb("RA", [P, K, NT, E], F32, rt)
        RB = sb("RB", [P, K, NT, E], F32, rt)
        U, ones = sb("U", [P, P], F32, rt), sb("ones", [P, P], F32, rt)
        m8, r8, w8 = sb("m8", [P, NT], F32, rt), sb("r8", [P, NT], F32, rt), sb("w8", [P, E], F32, rt)
        mx, pos = sb("mx", [P, K, NT], F32, rt), sb("pos", [P, K, NT], F32, rt)
        tok, row_s = sb("tok", [P, NT], I32, rt), sb("row_s", [P, K, NT], I32, rt)
        rt.close()
        X.append((sb("Xch", [P, DT, 256], F32R), sb("Xcl", [P, DT, 256], F32R)))
        zero_i = RA[:, :, :, :].rearrange("p k t e -> p (k t e)").bitcast(I32)[:, 0:E * ST]

        psH = [ctx.enter_context(nc.psum_tensor(f"c_psH{q}", [P, 512], F32)) for q in range(2)]
        psT = [ctx.enter_context(nc.psum_tensor(f"c_psT{q}", [P, DT, P], F32)) for q in range(2)]
        psY = [ctx.enter_context(nc.psum_tensor(f"c_psY{t}", [P, D], F32)) for t in range(BT)]

        s_raw = [sem(f"c_raw{q}") for q in range(RING)]
        s_xrow = [sem(f"c_xrow{q}") for q in range(2)]
        s_xg = [sem(f"c_gathered{q}") for q in range(2)]
        s_xts = [sem(f"c_xt_stored{q}") for q in range(2)]
        s_yst = [sem(f"c_y_stored{q}") for q in range(2)]
        s_whi, s_wlo, s_pad, s_gin, s_ghi, s_glo = (
            sem(f"c_{n}") for n in ("weights_hi", "weights_lo", "pad", "gate_in", "gate_hi", "gate_lo"))
        s_bin, s_bt, s_b1, s_b2, s_sd, s_rs, s_nm = (
            sem(f"c_{n}") for n in ("b1_in", "b1_turned", "b1", "b2", "std", "rstd", "nmr"))
        s_norm, s_T, s_xhi, s_xlo = (sem(f"c_{n}") for n in ("normed", "turned", "x_hi", "x_lo"))
        s_mm1, s_gelu, s_hhi, s_hlo, s_mm2, s_yev = (
            sem(f"c_{n}") for n in ("hidden", "gelu", "h_hi", "h_lo", "mm2", "y_out"))
        s_lT, s_lP, s_lg = (sem(f"c_{n}") for n in ("logits_T", "logits_turned", "logits"))
        s_rc, s_v, s_ex, s_cum, s_z, s_rows, s_sc, s_idx = (
            sem(f"c_{n}") for n in ("router_consts", "router_step", "router_exp", "cumulated",
                                    "table_cleared", "rows", "scattered", "slots_in"))
        s_b1e = sem("c_b1_expert")
        g_sp, g_pool, g_pe, g_act = (sem(f"c_gate_{n}") for n in ("sp", "pool", "pe", "act"))
        block = ctx.enter_context(nc.Block("experts"))

        def shared(b):
            return dict(B=b, t0=b * BT, th=b * (BT // 2), n=BT, gathered=False)

        def expert(e, k):
            o, n = EB[k]
            return dict(B=e * 3 + SB + k, t0=e * ST + NT + o, th=e * (ST // 2) + (NT + o) // 2, n=n,
                        gathered=True)

        X_OF = (2, 0, 1)

        def piece(wset, w_):
            W1, W2, WD, WU = wset
            r = raw[w_ % RING]
            if w_ < 2:
                a = slice(2 * w_, 2 * w_ + 2)
                v = r[:, 0:2 * LR].rearrange("p (a n) -> p a n", a=2)
                return WD.rearrange("(a p) n -> p a n", p=P)[:, a, :], v, L1h[:, a, 0:LR], L1l[:, a, 0:LR]
            if w_ < 4:
                a = slice((w_ - 2) * 256, (w_ - 1) * 256)
                return WU[:, a], r[0:LR, 0:256], L2h[:, a], L2l[:, a]
            j = (w_ - 4) // 2
            if w_ % 2 == 0:
                v = r[:, :].rearrange("p (a n) -> p a n", a=DT)
                return (W1.rearrange("(a p) f -> p a f", p=P)[:, :, j * P:(j + 1) * P], v,
                        W1h[:, j, :, :], W1l[:, j, :, :])
            return W2[j * P:(j + 1) * P, :], r[:, :], W2h[:, j, :], W2l[:, j, :]

        def pieces_of(j):
            return range(0, 4) if j == 0 else range(2 + 2 * j, 4 + 2 * j)

        def weights_of(e):
            def at(a):
                return a[bass.ds(e, 1), :, :].rearrange("o r c -> (o r) c")
            return at(w["w1"]), at(w["w2"]), at(w["wd"]), at(w["wu"])

        SHARED_W = (w["sw1"], w["sw2"], w["swd"], w["swu"])
        y_v = y_d.rearrange("(e p j) d -> e p j d", e=E, j=ST)

        @block.sync
        def _(sp):
            def load_chunk(s, wset, j):
                for w_ in pieces_of(j):
                    pass_gate(sp, s_wlo, s * PIECES + w_ - RING + 1, g_sp)
                    src, view, _, _ = piece(wset, w_)
                    sp.dma_start(view, src).then_inc(s_raw[w_ % RING], 16)

            def load_pieces(s, wset):
                for j in range(J):
                    load_chunk(s, wset, j)

            def row_in(b, t):
                at, q = shared(b), t % 2
                pass_gate(sp, s_T, at["t0"] + t - 1, g_sp)
                pass_gate(sp, s_xts[q], (at["th"] + t // 2) * 16, g_sp)
                sp.dma_start(xrow[q][:, :], x1_d[bass.ds(b * (BT * P) + t * P, P), :]).then_inc(s_xrow[q], 16)

            def row_out(b, t):
                q = t % 2
                pass_gate(sp, s_norm, b * BT + t + 1, g_sp)
                sp.dma_start(xt_d[bass.ds(b * (BT * P) + t * P, P), :], xrow[q][:, :]).then_inc(s_xts[q], 16)

            def rows(b):
                for t in range(BT):
                    row_in(b, t)
                    row_out(b, t)

            def store(at, dest):
                for t in range(at["n"]):
                    pass_gate(sp, s_yev, at["t0"] + t + 1, g_sp)
                    sp.dma_start(dest(t), yst[t % 2][:, :]).then_inc(s_yst[t % 2], 16)

            def store_shared(b):
                store(shared(b), lambda t: sh_d[bass.ds(b * (BT * P) + t * P, P), :])

            def store_expert(e, k):
                store(expert(e, k), lambda t: y_v[bass.ds(e, 1), :, EB[k][0] + t, :].rearrange("o p d -> (o p) d"))

            def bias2(e, at):
                pass_gate(sp, s_yev, at["t0"], g_sp)
                sp.dma_start(b2bc[:, :], w["b2"][bass.ds(e, 1), :].rearrange("o d -> (o d)").partition_broadcast(P))\
                    .then_inc(s_b2, 16)

            sp.dma_start(raw[0][:, 0:P], w["b1"].rearrange("e (c p) -> (e c) p", p=P)).then_inc(s_bin, 16)
            sp.dma_start(raw[1][0:FC, 0:P], w["sb1"].rearrange("(c p) -> c p", p=P)).then_inc(s_bin, 16)
            sp.dma_start(b2bc[:, :], w["sb2"].partition_broadcast(P)).then_inc(s_b2, 16)
            sp.dma_start(graw[:, :, :], w["gate"].rearrange("(a p) e -> p a e", p=P)).then_inc(s_gin, 16)
            rows(0)
            sp.wait_ge(s_bt, 2)
            for j in range(J):
                load_chunk(0, SHARED_W, j)
                if j - 2 in FRONT:
                    row_in(1, FRONT.index(j - 2))
                if j - 4 in FRONT:
                    row_out(1, FRONT.index(j - 4))
            row_out(1, BT - 1)
            with sp.Fori(1, SB - 1) as b:
                store_shared(b - 1)
                rows(b + 1)
            store_shared(SB - 2)
            load_pieces(1, weights_of(0))
            store_shared(SB - 1)
            bias2(0, expert(0, 0))
            store_expert(0, 0)
            store_expert(0, 1)

            def steady(e):
                load_pieces(e + 1, weights_of(e))
                store_expert(e - 1, 2)
                bias2(e, expert(e, 0))
                store_expert(e, 0)
                store_expert(e, 1)

            with sp.Fori(1, E) as e:
                steady(e)
            store_expert(E - 1, 2)
            for q in range(2):
                sp.wait_ge(s_yst[q], (NT + E * ST) // 2 * 16)
                sp.wait_ge(s_xts[q], NT // 2 * 16)

        @block.scalar
        def _(act):
            def convert(s, w_, used=None):
                _, view, hi, _ = piece(SHARED_W, w_)
                act.wait_ge(s_raw[w_ % RING], (s * (PIECES // RING) + w_ // RING + 1) * 16)
                if used is not None:
                    act.wait_ge(s_mm2, used)
                nc.scalar.copy(hi, view).then_inc(s_whi, 1)

            def convert_chunk(s, j, old=None):
                for w_ in pieces_of(j):
                    convert(s, w_, None if old is None else old["B"] * J + j + 1)

            def normalise(b, t):
                at = shared(b)
                pass_gate(act, s_xrow[t % 2], (at["th"] + t // 2 + 1) * 16, g_act)
                col = b * BT + t
                nc.scalar.activation(xrow[t % 2][:, :], xrow[t % 2][:, :], ACT.Identity,
                                     bias=nm1[:, bass.ds(col, 1)], scale=rs1[:, bass.ds(col, 1)]).then_inc(s_norm, 1)

            def x_hi(at, xb, used, t):
                act.wait_ge(s_T, at["t0"] + t + 1)
                if used is not None:
                    after(act, s_mm1, used)
                nc.scalar.copy(X[xb][0][:, :, t * P:(t + 1) * P], psT[t % 2][:, :, :]).then_inc(s_xhi, 1)

            def run(at, b1, logits=False, nxt=None, wset=None, lead=False):
                G, n = at["B"] * J, at["n"]
                for j in range(J):
                    if lead and j + LEAD < J:
                        convert_chunk(0, j + LEAD)
                    if nxt and nxt[3] and j + 1 in FRONT:
                        nxt[3](FRONT.index(j + 1))
                    act.wait_ge(s_mm1, G + j + 1)
                    after(act, s_hlo, G + j)
                    if j == 0:
                        nc.scalar.activation(h32[0:LR, 0:n * P], psH[0][0:LR, 0:n * P], ACT.Gelu).then_inc(s_gelu, 1)
                        if logits:
                            nc.scalar.copy(h32[LR:LR + E, :], psH[0][LR:LR + E, :]).then_inc(s_lT, 1)
                    else:
                        if logits and j == 1:
                            act.wait_ge(s_lP, at["B"] + 1)
                        nc.scalar.activation(h32[:, 0:n * P], psH[j % 2][:, 0:n * P], ACT.Gelu,
                                             bias=b1[:, j - 1:j]).then_inc(s_gelu, 1)
                    if nxt and j - 1 in FRONT and FRONT.index(j - 1) < nxt[0]["n"]:
                        x_hi(*nxt[:3], FRONT.index(j - 1))
                    if wset is not None and j >= LEAD:
                        convert_chunk(wset, j - LEAD, at)
                if wset is not None:
                    for j in range(J - LEAD, J):
                        convert_chunk(wset, j, at)

            nc.scalar.activation(rs1[:, :], mv1[:, :, 1], ACT.Sqrt, bias=eps[:, :]).then_inc(s_sd, 1)
            act.wait_ge(s_pad, 2)
            act.wait_ge(s_gin, 16)
            nc.scalar.copy(L1h[:, :, LR:LR + E], graw[:, :, :]).then_inc(s_ghi, 1)
            act.wait_ge(s_nm, 1)
            for t in range(BT):
                normalise(0, t)
                x_hi(shared(0), 0, None, t)
            act.wait_ge(s_bt, 1)
            nc.scalar.copy(b1T[:, 0:E * FC], psH[0][:, 0:E * FC]).then_inc(s_b1, 1)
            act.wait_ge(s_bt, 2)
            nc.scalar.copy(b1T[:, E * FC:], psH[1][:, 0:FC]).then_inc(s_b1, 1)
            act.wait_ge(s_b1, 2)
            for j in range(LEAD):
                convert_chunk(0, j)

            def shared_block(b, q, **more):
                run(shared(b), b1T[:, E * FC:], logits=True,
                    nxt=(shared(b + 1), 1 - q, b * J, lambda t: normalise(b + 1, t)), **more)

            shared_block(0, 0, lead=True)
            with act.Fori(0, SB // 2 - 1) as i:
                shared_block(i * 2 + 1, 1)
                shared_block(i * 2 + 2, 0)
            run(shared(SB - 1), b1T[:, E * FC:], logits=True, wset=1)
            act.wait_ge(s_v, 2)
            nc.scalar.activation(lg[:, :, :], lg[:, :, :], ACT.Exp).then_inc(s_ex, 1)
            for t in range(EB[0][1]):
                x_hi(expert(0, 0), X_OF[0], None, t)

            def expert_blocks(e, last=False):
                def nxt(e_, k):
                    return (expert(e_, k), X_OF[k], (expert(e_, k)["B"] - 2) * J, None)
                pass_gate(act, s_gelu, expert(e, 0)["B"] * J, g_act)
                nc.scalar.copy(b1e[:, :], b1T[:, bass.ds(e * FC, FC)]).then_inc(s_b1e, 1)
                act.wait_ge(s_b1e, e + 1)
                run(expert(e, 0), b1e, nxt=nxt(e, 1))
                run(expert(e, 1), b1e, nxt=nxt(e, 2))
                if last:
                    run(expert(e, 2), b1e)
                else:
                    run(expert(e, 2), b1e, nxt=nxt(e + 1, 0), wset=e + 2)

            with act.Fori(0, E - 1) as e:
                expert_blocks(e)
            expert_blocks(E - 1, last=True)

        @block.gpsimd
        def _(pool):
            def lows(s, j):
                for w_ in pieces_of(j):
                    _, view, hi, lo = piece(SHARED_W, w_)
                    pool.wait_ge(s_whi, s * PIECES + w_ + 1)
                    nc.gpsimd.tensor_tensor(lo, view, hi.bitcast(F32), ALU.subtract).then_inc(s_wlo, 1)

            def gather(e, k, t):
                at = expert(e, k)
                pass_gate(pool, s_T, at["t0"] + t - 1, g_pool)
                nc.gpsimd.indirect_dma_start(
                    out=xrow[t % 2][:, :], out_offset=None, in_=xt_d[:, :],
                    in_offset=bass.IndirectOffsetOnAxis(ap=idx[:, EB[k][0] + t:EB[k][0] + t + 1], axis=0),
                    bounds_check=T - 1).then_inc(s_xg[t % 2], 16)

            def slots(e):
                pass_gate(pool, s_T, expert(e, 0)["t0"], g_pool)
                pool.dma_start(idx[:, :], idx_d[bass.ds(e * SLOTS, SLOTS), :].rearrange("(p j) o -> p (j o)", j=ST))\
                    .then_inc(s_idx, 16)
                pass_gate(pool, s_idx, (e + 1) * 16, g_pool)

            nc.gpsimd.memzero(L1h[:, :, :]).then_inc(s_pad, 1)
            nc.gpsimd.memzero(L1l[:, :, :]).then_inc(s_pad, 1)
            nc.gpsimd.memset(U[:, :], 1.0).then_inc(s_rc, 1)
            nc.gpsimd.memset(ones[:, :], 1.0).then_inc(s_rc, 1)
            nc.gpsimd.iota(tok[:, :], [[P, NT]], base=0, channel_multiplier=1).then_inc(s_rc, 1)
            nc.gpsimd.memset(zero_i, 0).then_inc(s_rc, 1)
            for e in range(E):
                nc.gpsimd.memset(w8[:, e:e + 1], float(E - e)).then_inc(s_rc, 1)
            pool.wait_ge(s_rc, 4 + E)
            nc.gpsimd.affine_select(out=U[:, :], in_=U[:, :], compare_op=ALU.is_gt, fill=0.0,
                                    base=0, pattern=[[1, P]], channel_multiplier=-1).then_inc(s_rc, 1)
            pool.dma_start(idx_d.rearrange("(p j) o -> p (j o)", p=P), zero_i).then_inc(s_z, 16)
            pool.wait_ge(s_ghi, 1)
            nc.gpsimd.tensor_tensor(L1l[:, :, LR:LR + E], graw[:, :, :], L1h[:, :, LR:LR + E].bitcast(F32),
                                    ALU.subtract).then_inc(s_glo, 1)
            for j in range(J):
                lows(0, j)
            for j in range(J):
                lows(1, j)
            pool.wait_ge(s_rows, 1)
            pool.wait_ge(s_z, 16)
            for k in range(K):
                for t in range(NT):
                    nc.gpsimd.indirect_dma_start(
                        out=idx_d[:, :], out_offset=bass.IndirectOffsetOnAxis(ap=row_s[:, k, t:t + 1], axis=0),
                        in_=tok[:, t:t + 1], in_offset=None,
                        bounds_check=E * SLOTS - 1, oob_is_err=False).then_inc(s_sc, 16)
            pool.wait_ge(s_sc, K * NT * 16)
            for q in range(2):
                pool.wait_ge(s_xts[q], NT // 2 * 16)
            slots(0)
            for t in range(EB[0][1]):
                gather(0, 0, t)

            def steady(e, last=False):
                for k in (1, 2):
                    for t in range(EB[k][1]):
                        gather(e, k, t)
                if last:
                    return
                slots(e + 1)
                for t in range(EB[0][1]):
                    gather(e + 1, 0, t)
                for j in range(J):
                    lows(e + 2, j)

            with pool.Fori(0, E - 1) as e:
                steady(e)
            steady(E - 1, last=True)

        @block.vector
        def _(dve):
            def x_lo(at, xb, t):
                dve.wait_ge(s_xhi, at["t0"] + t + 1)
                cols = slice(t * P, (t + 1) * P)
                nc.vector.tensor_tensor(X[xb][1][:, :, cols], psT[t % 2][:, :, :], X[xb][0][:, :, cols].bitcast(F32),
                                        ALU.subtract).then_inc(s_xlo, 1)

            def run(at, bias_count, logits=False, nxt=None, extra=None):
                G, n = at["B"] * J, at["n"]
                for j in range(J):
                    rows = LR if j == 0 else P
                    a = (slice(0, rows), slice(0, n * P))
                    after(dve, s_mm2, G + j - 1 if j >= 2 else G)
                    dve.wait_ge(s_gelu, G + j + 1)
                    nc.vector.tensor_copy(hh[j % 2][a], h32[a]).then_inc(s_hhi, 1)
                    dve.wait_ge(s_hhi, G + j + 1)
                    nc.vector.tensor_tensor(hl[j % 2][a], h32[a], hh[j % 2][a].bitcast(F32), ALU.subtract)\
                        .then_inc(s_hlo, 1)
                    if logits and j == 0:
                        dve.wait_ge(s_lP, at["B"] + 1)
                        nc.vector.tensor_copy(lg[:, bass.ds(at["B"] * BT, BT), :],
                                              psH[0][:, 0:BT * E].rearrange("p (t e) -> p t e", e=E)).then_inc(s_lg, 1)
                    if nxt and j - 1 in FRONT and FRONT.index(j - 1) < nxt[0]["n"]:
                        x_lo(*nxt, FRONT.index(j - 1))
                    if extra and j == 1:
                        extra()
                dve.wait_ge(s_mm2, G + J)
                dve.wait_ge(s_b2, bias_count)
                for t in range(n):
                    after(dve, s_yst[t % 2], (at["th"] + t // 2) * 16)
                    nc.vector.tensor_tensor(yst[t % 2][:, :], psY[t][:, :], b2bc[:, :], ALU.add).then_inc(s_yev, 1)

            count = [0]

            def step(ins):
                count[0] += 1
                ins.then_inc(s_v, 1)
                dve.wait_ge(s_v, count[0])

            def over_e(a):
                return a.unsqueeze(2).to_broadcast([P, NT, E])

            def router():
                v = nc.vector
                dve.wait_ge(s_lg, SB)
                dve.wait_ge(s_rc, 5 + E)
                dve.wait_ge(s_z, 16)
                step(v.tensor_reduce(m8[:, :], lg[:, :, :], AXX, ALU.max))
                step(v.tensor_tensor(lg[:, :, :], lg[:, :, :], over_e(m8[:, :]), ALU.subtract))

            def router2():
                v = nc.vector
                dve.wait_ge(s_ex, 1)
                step(v.tensor_reduce(m8[:, :], lg[:, :, :], AXX, ALU.add))
                step(v.reciprocal(r8[:, :], m8[:, :]))
                step(v.tensor_tensor(lg[:, :, :], lg[:, :, :], over_e(r8[:, :]), ALU.mult))
                w8b = w8[:, :].unsqueeze(1).to_broadcast([P, NT, E])
                for k in range(K):
                    step(v.tensor_reduce(wgt[:, k, :], lg[:, :, :], AXX, ALU.max))
                    step(v.tensor_tensor(RB[:, k, :, :], lg[:, :, :], over_e(wgt[:, k, :]), ALU.is_equal))
                    step(v.tensor_tensor(RB[:, k, :, :], RB[:, k, :, :], w8b, ALU.mult))
                    step(v.tensor_reduce(mx[:, k, :], RB[:, k, :, :], AXX, ALU.max))
                    step(v.tensor_tensor(OH[:, k, :, :], RB[:, k, :, :], over_e(mx[:, k, :]), ALU.is_equal))
                    if k + 1 < K:
                        step(v.scalar_tensor_tensor(lg[:, :, :], OH[:, k, :, :], -2.0, lg[:, :, :],
                                                    ALU.mult, ALU.add))
                assert count[0] == PICKED
                dve.wait_ge(s_cum, 1)
                step(v.tensor_copy(RB[:, :, :, :].rearrange("p k t e -> p (k t e)"),
                                   psT[1][:, :, :].rearrange("p a b -> p (a b)")))
                for k in range(K):
                    for e in range(E):
                        step(v.tensor_tensor_scan(RA[:, k, :, e], ones[:, 0:NT], RB[:, k, :, e], 0.0,
                                                  ALU.mult, ALU.add))
                step(v.tensor_tensor(RA[:, :, :, :], RA[:, :, :, :], RB[:, :, :, :], ALU.subtract))
                step(v.tensor_tensor(RA[:, :, :, :].rearrange("p k t e -> p (k t e)"),
                                     RA[:, :, :, :].rearrange("p k t e -> p (k t e)"),
                                     psT[0][:, :, :].rearrange("p a b -> p (a b)"), ALU.add))
                step(v.tensor_tensor(RA[:, :, :, :], RA[:, :, :, :], OH[:, :, :, :], ALU.mult))
                step(v.tensor_reduce(pos[:, :, :].rearrange("p k t -> p (k t)"),
                                     RA[:, :, :, :].rearrange("p k t e -> p (k t) e"), AXX, ALU.add))
                keep, row, far = (RB[:, 0, i * 8:(i + 1) * 8, :].rearrange("p (k a) e -> p k (a e)", k=K)
                                  for i in range(3))
                step(v.tensor_scalar(keep, pos[:, :, :], float(CAP), None, ALU.is_lt))
                step(v.tensor_tensor(wgt[:, :, :], wgt[:, :, :], keep, ALU.mult))
                for k in range(K):
                    step(v.tensor_scalar(row[:, k, :], mx[:, k, :], -float(SLOTS), float(E * SLOTS + k * CAP),
                                         ALU.mult, ALU.add))
                step(v.tensor_tensor(row, row, pos[:, :, :], ALU.add))
                step(v.tensor_tensor(far, row, keep, ALU.mult))
                step(v.tensor_copy(row_g[:, :, :], far))
                step(v.tensor_scalar(far, keep, -float(E * SLOTS), float(E * SLOTS), ALU.mult, ALU.add))
                step(v.tensor_tensor(far, far, row, ALU.add))
                v.tensor_copy(row_s[:, :, :], far).then_inc(s_rows, 1)

            dve.wait_ge(s_sd, 1)
            nc.vector.reciprocal(rs1[:, :], rs1[:, :]).then_inc(s_rs, 1)
            dve.wait_ge(s_rs, 1)
            nc.vector.scalar_tensor_tensor(nm1[:, :], mv1[:, :, 0], -1.0, rs1[:, :], ALU.mult, ALU.mult)\
                .then_inc(s_nm, 1)
            for t in range(BT):
                x_lo(shared(0), 0, t)

            def shared_block(b, q):
                run(shared(b), 16, logits=True, nxt=(shared(b + 1), 1 - q))

            shared_block(0, 0)
            with dve.Fori(0, SB // 2 - 1) as i:
                shared_block(i * 2 + 1, 1)
                shared_block(i * 2 + 2, 0)
            run(shared(SB - 1), 16, logits=True, extra=router)
            router2()
            for t in range(EB[0][1]):
                x_lo(expert(0, 0), X_OF[0], t)

            def expert_blocks(e, last=False):
                run(expert(e, 0), (e + 2) * 16, nxt=(expert(e, 1), X_OF[1]))
                run(expert(e, 1), (e + 2) * 16, nxt=(expert(e, 2), X_OF[2]))
                run(expert(e, 2), (e + 2) * 16, nxt=None if last else (expert(e + 1, 0), X_OF[0]))

            with dve.Fori(0, E - 1) as e:
                expert_blocks(e)
            expert_blocks(E - 1, last=True)

        @block.tensor
        def _(pe):
            def turn(at, t):
                if at["gathered"]:
                    pe.wait_ge(s_xg[t % 2], (at["th"] - NT // 2 + t // 2 + 1) * 16)
                else:
                    pe.wait_ge(s_norm, at["t0"] + t + 1)
                after(pe, s_xlo, at["t0"] + t - 1)
                for d in range(DT):
                    last = nc.tensor.transpose(psT[t % 2][:, d, :], xrow[t % 2][:, d * P:(d + 1) * P], ident[:, :])
                last.then_inc(s_T, 1)

            def products(out, pairs):
                n = 3 * len(pairs)
                i = 0
                for (ah, al), (bh, bl) in pairs:
                    for a, b in ((ah, bh), (ah, bl), (al, bh)):
                        last = nc.tensor.matmul(out, a, b, start=(i == 0), stop=(i == n - 1))
                        i += 1
                return last

            def run(at, xb, s, logits=False, nxt=None):
                G, n = at["B"] * J, at["n"]
                Xh, Xl = X[xb]
                cols = slice(0, n * P)

                def up(j):
                    pe.wait_ge(s_wlo, s * PIECES + (4 if j == 0 else 4 + 2 * j))
                    after(pe, s_gelu, G + j - 1 if j >= 2 else G)
                    if j == 0:
                        pe.wait_ge(s_xlo, at["t0"] + n)
                        wh, wl = L1h, L1l
                        if logits:
                            pe.wait_ge(s_glo, 1)
                    else:
                        wh, wl = W1h[:, j - 1, :, :], W1l[:, j - 1, :, :]
                    if logits and j == 2:
                        pe.wait_ge(s_lg, at["B"] + 1)
                    products(psH[j % 2][:, cols], [((wh[:, d, :], wl[:, d, :]), (Xh[:, d, cols], Xl[:, d, cols]))
                                                   for d in range(DT)]).then_inc(s_mm1, 1)

                def down(j):
                    if j == 0:
                        after(pe, s_yev, at["t0"])
                    pe.wait_ge(s_hlo, G + j + 1)
                    rows = LR if j == 0 else P
                    wh, wl = (L2h, L2l) if j == 0 else (W2h[:, j - 1, :], W2l[:, j - 1, :])
                    for t in range(n):
                        c = slice(t * P, (t + 1) * P)
                        for i, (a, b) in enumerate(((hh, wh), (hh, wl), (hl, wh))):
                            last = nc.tensor.matmul(psY[t][:, :], a[j % 2][0:rows, c], b[0:rows, :],
                                                    start=(j == 0 and i == 0), stop=(j == J - 1 and i == 2))
                    last.then_inc(s_mm2, 1)

                up(0)
                for j in range(J):
                    if j + 1 < J:
                        up(j + 1)
                    if logits and j == 0:
                        pass_gate(pe, s_lT, at["B"] + 1, g_pe)
                        for t in range(BT):
                            last = nc.tensor.transpose(psH[0][:, t * E:(t + 1) * E],
                                                       h32[LR:LR + E, t * P:(t + 1) * P], ident[LR:LR + E, LR:LR + E])
                        last.then_inc(s_lP, 1)
                    if nxt and j in FRONT and FRONT.index(j) < nxt["n"]:
                        t = FRONT.index(j)
                        turn(nxt, t)
                    down(j)

            for t in range(BT):
                turn(shared(0), t)
            pe.wait_ge(s_bin, 32)
            nc.tensor.transpose(psH[0][:, 0:P], raw[0][:, 0:P], ident[:, :]).then_inc(s_bt, 1)
            nc.tensor.transpose(psH[1][:, 0:FC], raw[1][0:FC, 0:P], ident[0:FC, 0:FC]).then_inc(s_bt, 1)
            pe.wait_ge(s_b1, 2)

            def shared_block(b, q):
                run(shared(b), q, 0, logits=True, nxt=shared(b + 1))

            shared_block(0, 0)
            with pe.Fori(0, SB // 2 - 1) as i:
                shared_block(i * 2 + 1, 1)
                shared_block(i * 2 + 2, 0)
            run(shared(SB - 1), 1, 0, logits=True)
            pe.wait_ge(s_v, PICKED)
            pe.wait_ge(s_rc, 5 + E)
            flat = OH[:, :, :, :].rearrange("p k t e -> p (k t e)")
            nc.tensor.matmul(psT[0][:, :, :].rearrange("p a b -> p (a b)"), U[:, :], flat, start=True, stop=True)
            nc.tensor.matmul(psT[1][:, :, :].rearrange("p a b -> p (a b)"), ones[:, :], flat, start=True, stop=True)\
                .then_inc(s_cum, 1)
            pe.wait_ge(s_rows, 1)
            for t in range(EB[0][1]):
                turn(expert(0, 0), t)

            def expert_blocks(e, last=False):
                run(expert(e, 0), X_OF[0], e + 1, nxt=expert(e, 1))
                run(expert(e, 1), X_OF[1], e + 1, nxt=expert(e, 2))
                run(expert(e, 2), X_OF[2], e + 1, nxt=None if last else expert(e + 1, 0))

            with pe.Fori(0, E - 1) as e:
                expert_blocks(e)
            expert_blocks(E - 1, last=True)


def combine(nc, sem, const, x1_d, sh_d, y_d, out):
    wgt, row_g, eps = const["wgt"], const["row_g"], const["eps"]
    N = 4
    with ExitStack() as ctx:
        def ring(name, shape):
            return [ctx.enter_context(nc.sbuf_tensor(f"{name}{q}", shape, F32)) for q in range(N)]

        y0, y1, shr, x1r = ring("d_y0", [P, D]), ring("d_y1", [P, D]), ring("d_sh", [P, D]), ring("d_x1", [P, D])
        st, mv, sd, rs, nm = (ring(f"d_{n}", [P, k]) for n, k in
                              (("st", 6), ("mv", 2), ("sd", 1), ("rs", 1), ("nm", 1)))
        s_g = [sem(f"d_gathered{q}") for q in range(N)]
        s_l = [sem(f"d_loaded{q}") for q in range(N)]
        s_o = [sem(f"d_stored{q}") for q in range(N)]
        s_a, s_b, s_c, s_st, s_mv, s_sd, s_rs, s_nm, s_n, s_x = (
            sem(f"d_{n}") for n in ("w0y0", "w1y1", "sum", "stats", "meanvar", "std", "rstd", "nmr", "normed", "x2"))
        block = ctx.enter_context(nc.Block("combine"))

        @block.sync
        def _(sp):
            def store(t):
                sp.wait_ge(s_x, t + 1)
                sp.dma_start(out[t * P:(t + 1) * P, :], y0[t % N][:, :]).then_inc(s_o[t % N], 16)

            for t in range(NT):
                q = t % N
                after(sp, s_x, t - N + 1)
                sp.dma_start(shr[q][:, :], sh_d[t * P:(t + 1) * P, :]).then_inc(s_l[q], 16)
                sp.dma_start(x1r[q][:, :], x1_d[t * P:(t + 1) * P, :]).then_inc(s_l[q], 16)
                if t >= 2:
                    store(t - 2)
            store(NT - 2)
            store(NT - 1)
            for q in range(N):
                sp.wait_ge(s_o[q], NT // N * 16)

        @block.gpsimd
        def _(pool):
            for t in range(NT):
                q = t % N
                after(pool, s_o[q], t // N * 16)
                for k, dst in enumerate((y0, y1)):
                    nc.gpsimd.indirect_dma_start(
                        out=dst[q][:, :], out_offset=None, in_=y_d[:, :],
                        in_offset=bass.IndirectOffsetOnAxis(ap=row_g[:, k, t:t + 1], axis=0),
                        bounds_check=E * SLOTS - 1).then_inc(s_g[q], 16)

        @block.scalar
        def _(act):
            def norm(t):
                q = t % N
                act.wait_ge(s_mv, t + 1)
                nc.scalar.activation(sd[q][:, :], mv[q][:, 1:2], ACT.Sqrt, bias=eps[:, :]).then_inc(s_sd, 1)
                act.wait_ge(s_nm, t + 1)
                nc.scalar.activation(y0[q][:, :], y0[q][:, :], ACT.Identity, bias=nm[q][:, :], scale=rs[q][:, :])\
                    .then_inc(s_n, 1)

            for t in range(NT):
                q = t % N
                act.wait_ge(s_g[q], (t // N + 1) * 32)
                nc.scalar.mul(y0[q][:, :], y0[q][:, :], wgt[:, 0, t:t + 1]).then_inc(s_a, 1)
                if t >= 1:
                    norm(t - 1)
            norm(NT - 1)

        @block.vector
        def _(dve):
            v = nc.vector

            def add(t):
                q = t % N
                dve.wait_ge(s_a, t + 1)
                v.scalar_tensor_tensor(y0[q][:, :], y1[q][:, :], wgt[:, 1, t:t + 1], y0[q][:, :], ALU.mult, ALU.add)\
                    .then_inc(s_b, 1)
                dve.wait_ge(s_b, t + 1)
                dve.wait_ge(s_l[q], (t // N + 1) * 32)
                v.scalar_tensor_tensor(y0[q][:, :], shr[q][:, :], 0.2, y0[q][:, :], ALU.mult, ALU.add)\
                    .then_inc(s_c, 1)
                dve.wait_ge(s_c, t + 1)
                v.bn_stats(st[q][:, :], y0[q][:, :]).then_inc(s_st, 1)
                dve.wait_ge(s_st, t + 1)
                v.bn_aggr(mv[q][:, :], st[q][:, :]).then_inc(s_mv, 1)

            def scale(t):
                q = t % N
                dve.wait_ge(s_sd, t + 1)
                v.reciprocal(rs[q][:, :], sd[q][:, :]).then_inc(s_rs, 1)
                dve.wait_ge(s_rs, t + 1)
                v.scalar_tensor_tensor(nm[q][:, :], mv[q][:, 0:1], -1.0, rs[q][:, :], ALU.mult, ALU.mult)\
                    .then_inc(s_nm, 1)

            def residual(t):
                q = t % N
                dve.wait_ge(s_n, t + 1)
                v.tensor_tensor(y0[q][:, :], y0[q][:, :], x1r[q][:, :], ALU.add).then_inc(s_x, 1)

            for t in range(NT):
                add(t)
                if t >= 1:
                    scale(t - 1)
                if t >= 2:
                    residual(t - 2)
            scale(NT - 1)
            residual(NT - 2)
            residual(NT - 1)


_INS = dict(x="L0_attn_x", A_log="L0_attn_A_log", D_skip="L0_attn_D_skip", W_x="L0_attn_W_x", W_dt="L0_attn_W_dt",
            b_dt="L0_attn_b_dt", gate="L0_ffn_gate_w", w1="L0_ffn_w1", b1="L0_ffn_b1", w2="L0_ffn_w2", b2="L0_ffn_b2",
            wd="L0_ffn_wd", wu="L0_ffn_wu", sw1="L0_ffn_sw1", sb1="L0_ffn_sb1", sw2="L0_ffn_sw2", sb2="L0_ffn_sb2",
            swd="L0_ffn_swd", swu="L0_ffn_swu")


def program(nc, a, out):
    with ExitStack() as ctx:
        def sem(name):
            return ctx.enter_context(nc.semaphore(name))

        def dram(name, shape, dt=F32):
            return nc.dram_tensor(name, shape, dt).ap()

        dt_d, dtx_d = dram("dt_d", (DT, P, T)), dram("dtx_d", (DT, P, T))
        bc_d, skip_d = dram("bc_d", (2 * NS, T)), dram("skip_d", (T, D))
        x1_d, xt_d, sh_d = dram("x1_d", (T, D)), dram("xt_d", (T, D)), dram("sh_d", (T, D))
        y_d, idx_d = dram("y_d", (E * SLOTS, D)), dram("idx_d", (E * SLOTS, 1), I32)
        const = {n: ctx.enter_context(nc.sbuf_tensor(n, s, d)) for n, s, d in (
            ("ident", [P, P], F32), ("eps", [P, 1], F32), ("mv_x1", [P, NT, 2], F32),
            ("wgt", [P, K, NT], F32), ("row_g", [P, K, NT], I32))}
        with nc.sbuf_tensor("A_neg", [P, DT, NS], F32) as const["A_neg"]:
            prepare(nc, sem, const, a["x"], a["A_log"], a["D_skip"], a["W_x"], a["W_dt"], a["b_dt"],
                    dt_d, dtx_d, bc_d, skip_d)
            scan(nc, sem, const, a["x"], dt_d, dtx_d, bc_d, skip_d, x1_d)
        experts(nc, sem, const, a, x1_d, xt_d, sh_d, y_d, idx_d)
        combine(nc, sem, const, x1_d, sh_d, y_d, out)


def kernel(**inputs):
    import numpy as np
    import concourse.bacc as bacc
    from concourse.bass_utils import run_bass_kernel_spmd

    nc = bacc.Bacc("TRN2", target_bir_lowering=False, num_devices=1)
    arrays = {short: np.ascontiguousarray(inputs[name]) for short, name in _INS.items()}
    arrays["x"] = arrays["x"].reshape(T, D)
    arrays = {f"in_{short}": v for short, v in arrays.items()}
    aps = {n[3:]: nc.dram_tensor(n, v.shape, F32, kind="ExternalInput").ap() for n, v in arrays.items()}
    out = nc.dram_tensor("out", (T, D), F32, kind="ExternalOutput").ap()
    program(nc, aps, out)
    r = run_bass_kernel_spmd(nc, [arrays], core_ids=[0])
    return r.results[0]["out"].reshape(1, T, D)
```

```python
from contextlib import ExitStack

import concourse.bass as bass
from concourse import mybir

F32 = mybir.dt.float32
F32R = mybir.dt.float32r
I32 = mybir.dt.int32
ALU = mybir.AluOpType
ACT = mybir.ActivationFunctionType
AXX = mybir.AxisListType.X

P = 128
T, D = 4096, 512
NS, RANK = 16, 64
DT = D // P
CH = 512
CT = CH // P
NCH = T // CH
NT = T // P
E, K = 8, 2
CAP = int(T * 1.25 / E)
SLOTS = K * CAP
FF, LR = 4 * D, 32
FC = FF // P
EPS = 1e-5


def after(eng, sem, value):
    if isinstance(value, int) and value <= 0:
        return
    eng.wait_ge(sem, value)


def pass_gate(eng, sem, value, gate):
    after(eng, sem, value)
    eng.sem_inc(gate, 1)


def in_pairs(eng, body, first, last, peel=1):
    for i in range(first, first + peel):
        body(i, 0)
        body(i, 1)
    with eng.Fori(first + peel, last) as i:
        body(i, 0)
        body(i, 1)


def back(i, q, n):
    m = q - n
    i = i + m // 2
    return None if isinstance(i, int) and i < 0 else (i, m % 2)


def staged(eng, *stages):
    def body(i, q):
        for lag, f in stages:
            at = back(i, q, lag)
            if at is not None:
                f(*at)

    in_pairs(eng, body, 0, NCH // 2, 2)
    for c in range(NCH, NCH + max(lag for lag, _ in stages)):
        for lag, f in stages:
            if c - lag < NCH:
                f((c - lag) // 2, (c - lag) % 2)


def prepare(nc, sem, const, x, A_log, D_skip, W_x, W_dt, b_dt, dt_d, dtx_d, bc_d, skip_d):
    ident, A_neg, eps = const["ident"], const["A_neg"], const["eps"]
    NX = RANK + 2 * NS
    with ExitStack() as ctx:
        def sb(name, shape, dt=F32):
            return ctx.enter_context(nc.sbuf_tensor(name, shape, dt))

        def two(name, shape):
            return [sb(f"{name}{q}", shape) for q in range(2)]

        wx = sb("wx", [P, DT, NX])
        wdt = sb("wdt", [RANK, D])
        bdt = sb("bdt", [P, DT])
        alog = sb("alog", [P, DT, NS])
        dbc = sb("dbc", [P, D])
        xin, xn, xnT = two("xin", [P, CT, D]), two("xn", [P, CT, D]), two("xnT", [P, DT, CH])
        st, mv = two("st", [P, CT, 6]), two("mv", [P, CT, 2])
        sd, rstd, nmr = two("sd", [P, CT]), two("rstd", [P, CT]), two("nmr", [P, CT])
        xpT = two("xpT", [NX, CH])
        au = two("au", [P, DT, CH])
        w1 = two("w1", [P, DT, CH])
        lg = two("lg", [P, DT, CH])
        rz = two("rz", [P, DT, CH])
        dx = two("dx", [P, DT, CH])
        sk = two("sk", [P, CT, D])
        psT = [ctx.enter_context(nc.psum_tensor(f"a_psT{q}", [P, CH], F32)) for q in range(2)]
        psX = ctx.enter_context(nc.psum_tensor("a_psX", [P, CH], F32))
        psZ = ctx.enter_context(nc.psum_tensor("a_psZ", [P, DT, CH], F32))

        s_w, s_alog = sem("a_weights"), sem("a_alog_in")
        s_ident0, s_ident, s_eps = sem("a_ident_zero"), sem("a_ident"), sem("a_eps")
        s_ea, s_A = sem("a_expA"), sem("a_A")
        s_xin = [sem(f"a_x_in{q}") for q in range(2)]
        s_st, s_mv, s_sd, s_rs, s_nm = (sem(f"a_{n}") for n in ("stats", "meanvar", "std", "rstd", "nmr"))
        s_xn, s_xT, s_xnT, s_xp, s_xpT, s_z = (
            sem(f"a_{n}") for n in ("normed", "transposed", "xnT", "xp", "xpT", "z"))
        s_rz, s_az, s_u, s_w1, s_lg, s_d, s_a, s_n, s_dt, s_dx, s_sk = (
            sem(f"a_{n}") for n in ("z_out", "absz", "u", "w1", "ln", "w1_less_1", "relu_ln", "rest", "dt", "dtx", "skip"))
        g_sp, g_pool, g_dve = (sem(f"a_gate_{n}") for n in ("sp", "pool", "dve"))
        s_out = [sem(f"a_stored{q}") for q in range(2)]
        STORES = 5 * 16
        block = ctx.enter_context(nc.Block("prepare"))

        @block.sync
        def _(sp):
            def load(i, q):
                c = i * 2 + q
                pass_gate(sp, s_xn, (c - 1) * CT, g_sp)
                sp.dma_start(xin[q][:, :, :], x[bass.ds(c * CH, CH), :].rearrange("(t p) d -> p t d", p=P))\
                    .then_inc(s_xin[q], 16)

            def store(i, q):
                c = i * 2 + q
                cols = bass.ds(c * CH, CH)
                pass_gate(sp, s_xpT, c + 1, g_sp)
                sp.dma_start(bc_d[:, cols], xpT[q][RANK:NX, :]).then_inc(s_out[q], 16)
                pass_gate(sp, s_sk, (c + 1) * CT, g_sp)
                sp.dma_start(skip_d[bass.ds(c * CH, CH), :].rearrange("(t p) d -> p t d", p=P), sk[q][:, :, :])\
                    .then_inc(s_out[q], 16)
                pass_gate(sp, s_dt, c + 1, g_sp)
                sp.dma_start(dt_d[:, :, cols].rearrange("a p t -> p a t"), lg[q][:, :, :]).then_inc(s_out[q], 16)
                pass_gate(sp, s_dx, c + 1, g_sp)
                for h in range(2):
                    sp.dma_start(dtx_d[2 * h:2 * h + 2, :, cols].rearrange("a p t -> p a t"),
                                 dx[q][:, 2 * h:2 * h + 2, :]).then_inc(s_out[q], 16)

            staged(sp, (0, load), (3, store))
            for q in range(2):
                sp.wait_ge(s_out[q], STORES * NCH // 2)

        @block.gpsimd
        def _(pool):
            nc.gpsimd.memset(ident[:, :], 0.0).then_inc(s_ident0, 1)
            nc.gpsimd.memset(eps[:, :], EPS).then_inc(s_eps, 1)
            pool.wait_ge(s_ident0, 1)
            nc.gpsimd.affine_select(out=ident[:, :], in_=ident[:, :], compare_op=ALU.not_equal, fill=1.0,
                                    base=0, pattern=[[-1, P]], channel_multiplier=1).then_inc(s_ident, 1)
            pool.wait_ge(s_w, 64)

            def skip(i, q):
                c = i * 2 + q
                pool.wait_ge(s_xn, (c + 1) * CT)
                after(pool, s_out[q], i * STORES)
                for t in range(CT):
                    nc.gpsimd.tensor_tensor(sk[q][:, t, :], xn[q][:, t, :], dbc[:, :], ALU.mult).then_inc(s_sk, 1)

            def rest(i, q):
                c = i * 2 + q
                pool.wait_ge(s_d, c + 1)
                nc.gpsimd.tensor_tensor(au[q][:, :, :], au[q][:, :, :], w1[q][:, :, :], ALU.subtract).then_inc(s_n, 1)
                pool.wait_ge(s_a, c + 1)
                pool.wait_ge(s_n, c + 1)
                nc.gpsimd.tensor_tensor(lg[q][:, :, :], rz[q][:, :, :], au[q][:, :, :], ALU.add).then_inc(s_dt, 1)

            staged(pool, (1, skip), (2, rest))

        @block.scalar
        def _(act):
            with nc.allow_non_contiguous_dma(reason="512 biases"):
                act.dma_start(bdt[:, :], b_dt.rearrange("(t p) -> p t", p=P)).then_inc(s_w, 16)
            act.dma_start(wx[:, :, :], W_x.rearrange("(t p) n -> p t n", p=P)).then_inc(s_w, 16)
            act.dma_start(wdt[:, :], W_dt).then_inc(s_w, 16)
            act.dma_start(dbc[:, :], D_skip.partition_broadcast(P)).then_inc(s_w, 16)
            act.dma_start(alog[:, :, :], A_log.rearrange("(t p) n -> p t n", p=P)).then_inc(s_alog, 16)
            act.wait_ge(s_alog, 16)
            nc.scalar.activation(A_neg[:, :, :], alog[:, :, :], ACT.Exp).then_inc(s_ea, 1)
            act.wait_ge(s_eps, 1)
            act.wait_ge(s_w, 64)

            def norm(i, q):
                c = i * 2 + q
                act.wait_ge(s_mv, (c + 1) * CT)
                nc.scalar.activation(sd[q][:, :], mv[q][:, :, 1], ACT.Sqrt, bias=eps[:, :]).then_inc(s_sd, 1)
                act.wait_ge(s_nm, c + 1)
                after(act, s_sk, (c - 1) * CT)
                after(act, s_xT, (c - 1) * DT)
                for t in range(CT):
                    nc.scalar.activation(xn[q][:, t, :], xin[q][:, t, :], ACT.Identity, bias=nmr[q][:, t:t + 1],
                                         scale=rstd[q][:, t:t + 1]).then_inc(s_xn, 1)

            def project(i, q):
                c = i * 2 + q
                act.wait_ge(s_xp, c + 1)
                after(act, s_z, c - 1)
                after(act, s_out[q], i * STORES)
                nc.scalar.copy(xpT[q][:, :], psX[0:NX, :]).then_inc(s_xpT, 1)

            def decay(i, q):
                c = i * 2 + q
                act.wait_ge(s_rz, (c + 1) * DT)
                after(act, s_dt, c - 1)
                nc.scalar.activation(au[q][:, :, :], rz[q][:, :, :], ACT.Abs).then_inc(s_az, 1)
                act.wait_ge(s_az, c + 1)
                nc.scalar.activation(au[q][:, :, :], au[q][:, :, :], ACT.Exp, scale=-1.0).then_inc(s_u, 1)

            def log(i, q):
                c = i * 2 + q
                act.wait_ge(s_w1, c + 1)
                after(act, s_dx, c - 1)
                after(act, s_out[q], i * STORES)
                nc.scalar.activation(lg[q][:, :, :], w1[q][:, :, :], ACT.Ln).then_inc(s_lg, 1)

            staged(act, (2, decay), (0, norm), (1, project), (2, log))

        @block.vector
        def _(dve):
            dve.wait_ge(s_ea, 1)
            nc.vector.tensor_scalar(A_neg[:, :, :], A_neg[:, :, :], -1.0, None, ALU.mult).then_inc(s_A, 1)
            dve.wait_ge(s_w, 64)

            def stats(i, q):
                c = i * 2 + q
                dve.wait_ge(s_xin[q], (i + 1) * 16)
                for t in range(CT):
                    nc.vector.bn_stats(st[q][:, t, :], xin[q][:, t, :]).then_inc(s_st, 1)
                after(dve, s_sd, c - 1)
                for t in range(CT):
                    pass_gate(dve, s_st, c * CT + t + 1, g_dve)
                    nc.vector.bn_aggr(mv[q][:, t, :], st[q][:, t, :]).then_inc(s_mv, 1)

            def scale(i, q):
                c = i * 2 + q
                dve.wait_ge(s_sd, c + 1)
                after(dve, s_xn, (c - 1) * CT)
                nc.vector.reciprocal(rstd[q][:, :], sd[q][:, :]).then_inc(s_rs, 1)
                dve.wait_ge(s_rs, c + 1)
                dve.wait_ge(s_mv, (c + 1) * CT)
                nc.vector.scalar_tensor_tensor(nmr[q][:, :], mv[q][:, :, 0], -1.0, rstd[q][:, :], ALU.mult, ALU.mult)\
                    .then_inc(s_nm, 1)

            def evacuate(i, q):
                c = i * 2 + q
                after(dve, s_xp, c - 1)
                after(dve, s_dx, c - 1)
                for t in range(DT):
                    dve.wait_ge(s_xT, c * DT + t + 1)
                    nc.vector.tensor_copy(xnT[q][:, t, :], psT[t % 2][:, :]).then_inc(s_xnT, 1)

            def take_z(i, q):
                c = i * 2 + q
                dve.wait_ge(s_z, c + 1)
                after(dve, s_dt, c - 1)
                for t in range(DT):
                    nc.vector.tensor_scalar(rz[q][:, t, :], psZ[:, t, :], bdt[:, t:t + 1], None, ALU.add)\
                        .then_inc(s_rz, 1)

            def one_plus(i, q):
                c = i * 2 + q
                dve.wait_ge(s_u, c + 1)
                after(dve, s_n, c - 1)
                nc.vector.tensor_scalar(w1[q][:, :, :], au[q][:, :, :], 1.0, None, ALU.add).then_inc(s_w1, 1)

            def logs(i, q):
                c = i * 2 + q
                dve.wait_ge(s_lg, c + 1)
                nc.vector.tensor_scalar(w1[q][:, :, :], w1[q][:, :, :], -1.0, None, ALU.add).then_inc(s_d, 1)
                nc.vector.scalar_tensor_tensor(rz[q][:, :, :], rz[q][:, :, :], 0.0, lg[q][:, :, :], ALU.max, ALU.add)\
                    .then_inc(s_a, 1)

            def product(i, q):
                c = i * 2 + q
                dve.wait_ge(s_dt, c + 1)
                nc.vector.tensor_tensor(dx[q][:, :, :], lg[q][:, :, :], xnT[q][:, :, :], ALU.mult).then_inc(s_dx, 1)

            staged(dve, (2, take_z), (0, stats), (3, product), (1, evacuate), (0, scale), (2, one_plus), (2, logs))

        @block.tensor
        def _(pe):
            pe.wait_ge(s_ident, 1)
            pe.wait_ge(s_w, 64)

            def body(i, q):
                c = i * 2 + q
                pe.wait_ge(s_xn, (c + 1) * CT)
                for d in range(DT):
                    after(pe, s_xnT, c * DT + d - 1)
                    for t in range(CT):
                        last = nc.tensor.transpose(psT[d % 2][:, t * P:(t + 1) * P],
                                                   xn[q][:, t, d * P:(d + 1) * P], ident[:, :])
                    last.then_inc(s_xT, 1)
                after(pe, s_xpT, c)
                for d in range(DT):
                    pe.wait_ge(s_xnT, c * DT + d + 1)
                    last = nc.tensor.matmul(psX[0:NX, :], wx[:, d, :], xnT[q][:, d, :],
                                            start=(d == 0), stop=(d == DT - 1))
                last.then_inc(s_xp, 1)
                pe.wait_ge(s_xpT, c + 1)
                after(pe, s_rz, c * DT)
                for d in range(DT):
                    last = nc.tensor.matmul(psZ[:, d, :], wdt[:, d * P:(d + 1) * P], xpT[q][0:RANK, :],
                                            start=True, stop=True)
                last.then_inc(s_z, 1)

            staged(pe, (1, body))


def scan(nc, sem, const, x, dt_d, dtx_d, bc_d, skip_d, x1_d):
    ident, A_neg, eps, mv1 = const["ident"], const["A_neg"], const["eps"], const["mv_x1"]
    NU = NS * DT
    NU_, NH_, NP_ = 3, 6, 6
    with ExitStack() as ctx:
        def sb(name, shape, dt=F32):
            return ctx.enter_context(nc.sbuf_tensor(name, shape, dt))

        def two(name, shape):
            return [sb(f"{name}{q}", shape) for q in range(2)]

        dts, dtx = two("dts", [P, DT, CH]), two("dtxs", [P, DT, CH])
        Bs = two("Bs", [NS, CH])
        Cb = two("Cb", [P, NS, CH])
        skp, xr = two("skp", [P, CT, D]), two("xr", [P, CT, D])
        u = [sb(f"u{k}", [P, CH]) for k in range(NU_)]
        h = [sb(f"h{k}", [P, CH]) for k in range(NH_)]
        pr = [sb(f"pr{k}", [P, CH]) for k in range(NP_)]
        carry = sb("carry", [P, NU])
        sel = sb("sel", [NS, NS, P])
        ys = sb("ys", [P, CT, D])
        yo = two("yo", [P, CT, D])
        st, mv = sb("b_st", [P, CT, 6]), sb("b_mv", [P, CT, 2])
        st2, mv2 = sb("b_st2", [P, CT, 6]), sb("b_mv2", [P, CT, 2])
        sd, rstd, nmr = sb("b_sd", [P, CT]), sb("b_rstd", [P, CT]), sb("b_nmr", [P, CT])
        psA = [ctx.enter_context(nc.psum_tensor(f"b_psA{q}", [P, CH], F32)) for q in range(2)]
        psB = [ctx.enter_context(nc.psum_tensor(f"b_psB{q}", [P, CH], F32)) for q in range(2)]
        psY = [ctx.enter_context(nc.psum_tensor(f"b_psY{t}", [P, D], F32)) for t in range(CT)]

        s_ld = [sem(f"b_loaded{q}") for q in range(2)]
        s_pl = [sem(f"b_post_loaded{q}") for q in range(2)]
        s_sel0, s_sel, s_c0 = sem("b_sel_zero"), sem("b_sel"), sem("b_carry_zero")
        s_dA, s_bb, s_u, s_h, s_ca, s_p, s_y = (
            sem(f"b_{n}") for n in ("dA", "B_spread", "u", "h", "carry", "hC", "y_added"))
        s_ys, s_st, s_mv, s_sd, s_rs, s_nm, s_yn, s_x1, s_st2, s_mv2, s_mv1 = (
            sem(f"b_{n}") for n in ("y_out", "stats", "meanvar", "std", "rstd", "nmr", "normed", "x1", "stats2", "meanvar2", "meanvar_x1"))
        g_sp, g_dve = sem("b_gate_sp"), sem("b_gate_dve")
        s_out = [sem(f"b_stored{q}") for q in range(2)]
        block = ctx.enter_context(nc.Block("scan"))

        @block.sync
        def _(sp):
            def load(i, q):
                c = i * 2 + q
                cols = bass.ds(c * CH, CH)
                pass_gate(sp, s_p, (c - 1) * NU, g_sp)
                sp.dma_start(dts[q][:, :, :], dt_d[:, :, cols].rearrange("a p t -> p a t")).then_inc(s_ld[q], 16)
                sp.dma_start(Bs[q][:, :], bc_d[0:NS, cols]).then_inc(s_ld[q], 16)
                sp.dma_start(dtx[q][:, :, :], dtx_d[:, :, cols].rearrange("a p t -> p a t")).then_inc(s_ld[q], 16)
                sp.dma_start(Cb[q][:, :, :], bc_d[NS:2 * NS, cols].partition_broadcast(P)).then_inc(s_ld[q], 16)
                if not (isinstance(i, int) and i == 0):
                    store(i - 1, q)
                    pass_gate(sp, s_out[q], i * 16, g_sp)
                rows = bass.ds(c * CH, CH)
                sp.dma_start(skp[q][:, :, :], skip_d[rows, :].rearrange("(t p) d -> p t d", p=P))\
                    .then_inc(s_pl[q], 16)
                sp.dma_start(xr[q][:, :, :], x[rows, :].rearrange("(t p) d -> p t d", p=P)).then_inc(s_pl[q], 16)

            def store(i, q):
                c = i * 2 + q
                pass_gate(sp, s_x1, (c + 1) * CT, g_sp)
                sp.dma_start(x1_d[bass.ds(c * CH, CH), :].rearrange("(t p) d -> p t d", p=P), yo[q][:, :, :])\
                    .then_inc(s_out[q], 16)

            in_pairs(sp, load, 0, NCH // 2)
            store(NCH // 2 - 1, 0)
            store(NCH // 2 - 1, 1)
            for q in range(2):
                sp.wait_ge(s_out[q], 16 * NCH // 2)

        @block.scalar
        def _(act):
            def decay(c, q, k):
                n, d = k // DT, k % DT
                after(act, s_h, c * NU + k - 1)
                nc.scalar.activation(psA[k % 2][:, :], dts[q][:, d, :], ACT.Exp,
                                     scale=A_neg[:, d, n:n + 1]).then_inc(s_dA, 1)

            def keep(c, k):
                act.wait_ge(s_h, c * NU + k + 1)
                nc.scalar.copy(carry[:, k:k + 1], h[(k % NH_)][:, CH - 1:CH]).then_inc(s_ca, 1)

            def std(c):
                act.wait_ge(s_mv, (c + 1) * CT)
                nc.scalar.activation(sd[:, :], mv[:, :, 1], ACT.Sqrt, bias=eps[:, :]).then_inc(s_sd, 1)

            def norm(c, q):
                act.wait_ge(s_nm, c + 1)
                for t in range(CT):
                    nc.scalar.activation(yo[q][:, t, :], ys[:, t, :], ACT.Identity, bias=nmr[:, t:t + 1],
                                         scale=rstd[:, t:t + 1]).then_inc(s_yn, 1)

            act.wait_ge(s_c0, 1)

            def body(i, q):
                c = i * 2 + q
                post = not (isinstance(i, int) and i == 0 and q == 0)
                act.wait_ge(s_ld[q], (i + 1) * 64)
                decay(c, q, 0)
                decay(c, q, 1)
                for k in range(NU):
                    keep(c, k)
                    if k + 2 < NU:
                        decay(c, q, k + 2)
                    if post and k == 16:
                        std(c - 1)
                    if post and k == 22:
                        norm(c - 1, 1 - q)

            in_pairs(act, body, 0, NCH // 2)
            std(NCH - 1)
            norm(NCH - 1, 1)

        @block.vector
        def _(dve):
            nc.vector.memset(carry[:, :], 0.0).then_inc(s_c0, 1)

            def drive(c, q, k):
                n, d = k // DT, k % DT
                dve.wait_ge(s_bb, c * NS + n + 1)
                after(dve, s_h, c * NU + k - NU_ + 1)
                nc.vector.tensor_tensor(u[k % NU_][:, :], dtx[q][:, d, :], psB[n % 2][:, :], ALU.mult).then_inc(s_u, 1)

            def recur(c, k):
                g = c * NU + k
                dve.wait_ge(s_dA, g + 1)
                dve.wait_ge(s_u, g + 1)
                if k >= NH_:
                    dve.wait_ge(s_p, g - NH_ + 1)
                    dve.wait_ge(s_ca, g - NH_ + 1)
                else:
                    after(dve, s_p, c * NU)
                    after(dve, s_ca, c * NU)
                nc.vector.tensor_tensor_scan(h[k % NH_][:, :], psA[k % 2][:, :], u[k % NU_][:, :],
                                             carry[:, k:k + 1], ALU.mult, ALU.add).then_inc(s_h, 1)

            def take(c, q):
                dve.wait_ge(s_pl[q], (c - q) * 16 + 32)
                dve.wait_ge(s_y, (c + 1) * NU)
                after(dve, s_yn, c * CT)
                for t in range(CT):
                    nc.vector.tensor_tensor(ys[:, t, :], psY[t][:, :], skp[q][:, t, :], ALU.add).then_inc(s_ys, 1)

            def stats(c):
                dve.wait_ge(s_ys, (c + 1) * CT)
                for t in range(CT):
                    nc.vector.bn_stats(st[:, t, :], ys[:, t, :]).then_inc(s_st, 1)

            def aggregate(c):
                after(dve, s_sd, c)
                pass_gate(dve, s_st, (c + 1) * CT, g_dve)
                for t in range(CT):
                    nc.vector.bn_aggr(mv[:, t, :], st[:, t, :]).then_inc(s_mv, 1)

            def scale(c):
                dve.wait_ge(s_sd, c + 1)
                after(dve, s_yn, c * CT)
                nc.vector.reciprocal(rstd[:, :], sd[:, :]).then_inc(s_rs, 1)
                dve.wait_ge(s_rs, c + 1)
                nc.vector.scalar_tensor_tensor(nmr[:, :], mv[:, :, 0], -1.0, rstd[:, :], ALU.mult, ALU.mult)\
                    .then_inc(s_nm, 1)

            def residual(c, q):
                dve.wait_ge(s_yn, (c + 1) * CT)
                for t in range(CT):
                    nc.vector.tensor_tensor(yo[q][:, t, :], yo[q][:, t, :], xr[q][:, t, :], ALU.add).then_inc(s_x1, 1)

            def stats_x1(c, q):
                dve.wait_ge(s_x1, (c + 1) * CT)
                for t in range(CT):
                    nc.vector.bn_stats(st2[:, t, :], yo[q][:, t, :]).then_inc(s_st2, 1)

            def aggregate_x1(c):
                pass_gate(dve, s_st2, (c + 1) * CT, g_dve)
                for t in range(CT):
                    nc.vector.bn_aggr(mv2[:, t, :], st2[:, t, :]).then_inc(s_mv2, 1)
                dve.wait_ge(s_mv2, (c + 1) * CT)
                nc.vector.tensor_copy(mv1[:, bass.ds(c * CT, CT), :], mv2[:, :, :]).then_inc(s_mv1, 1)

            def body(i, q):
                c = i * 2 + q
                post = not (isinstance(i, int) and i == 0 and q == 0)
                dve.wait_ge(s_ld[q], (i + 1) * 64)
                drive(c, q, 0)
                for k in range(NU):
                    if k + 1 < NU:
                        drive(c, q, k + 1)
                    recur(c, k)
                    if post and k == 2:
                        take(c - 1, 1 - q)
                    if post and k == 8:
                        stats(c - 1)
                    if post and k == 12:
                        aggregate(c - 1)
                    if post and k == 20:
                        scale(c - 1)
                    if post and k == 30:
                        residual(c - 1, 1 - q)
                    if post and k == 36:
                        stats_x1(c - 1, 1 - q)
                    if post and k == 42:
                        aggregate_x1(c - 1)

            in_pairs(dve, body, 0, NCH // 2)
            take(NCH - 1, 1)
            stats(NCH - 1)
            aggregate(NCH - 1)
            scale(NCH - 1)
            residual(NCH - 1, 1)
            stats_x1(NCH - 1, 1)
            aggregate_x1(NCH - 1)

        @block.gpsimd
        def _(pool):
            nc.gpsimd.memset(sel[:, :, :], 0.0).then_inc(s_sel0, 1)
            pool.wait_ge(s_sel0, 1)
            nc.gpsimd.affine_select(out=sel[:, :, :], in_=sel[:, :, :], compare_op=ALU.not_equal, fill=1.0,
                                    base=0, pattern=[[-1, NS], [0, P]], channel_multiplier=1).then_inc(s_sel, 1)

            def body(i, q):
                c = i * 2 + q
                pool.wait_ge(s_ld[q], (i + 1) * 64)
                for k in range(NU):
                    g = c * NU + k
                    pool.wait_ge(s_h, g + 1)
                    if k >= NP_:
                        pool.wait_ge(s_y, g - NP_ + 1)
                    else:
                        after(pool, s_y, c * NU)
                    nc.gpsimd.tensor_tensor(pr[k % NP_][:, :], h[k % NH_][:, :], Cb[q][:, k // DT, :], ALU.mult)\
                        .then_inc(s_p, 1)

            in_pairs(pool, body, 0, NCH // 2)

        @block.tensor
        def _(pe):
            pe.wait_ge(s_sel, 1)

            def spread(c, q, n):
                if n >= 2:
                    pe.wait_ge(s_u, c * NU + (n - 1) * DT)
                else:
                    after(pe, s_u, c * NU)
                nc.tensor.matmul(psB[n % 2][:, :], sel[:, n, :], Bs[q][:, :], start=True, stop=True).then_inc(s_bb, 1)

            def body(i, q):
                c = i * 2 + q
                pe.wait_ge(s_ld[q], (i + 1) * 64)
                spread(c, q, 0)
                spread(c, q, 1)
                for k in range(NU):
                    n, d = k // DT, k % DT
                    if k == 0:
                        after(pe, s_ys, c * CT)
                    pe.wait_ge(s_p, c * NU + k + 1)
                    for t in range(CT):
                        last = nc.tensor.matmul(psY[t][:, d * P:(d + 1) * P], pr[k % NP_][:, t * P:(t + 1) * P],
                                                ident[:, :], start=(k == 0), stop=(k == NU - 1),
                                                skip_group_check=True)
                    last.then_inc(s_y, 1)
                    if d == DT - 1 and n + 2 < NS:
                        spread(c, q, n + 2)

            in_pairs(pe, body, 0, NCH // 2)


J = FC + 1
BT = 4
SB = T // (BT * P)
ST = SLOTS // P
EB = ((0, 2), (2, 4), (6, 4))
PIECES = 4 + 2 * FC
L3 = 3 * LR
RING = 4
FRONT = (2, 6, 10, 14)
HOT = 4
PICKED = 4 + 6 * K
LEAD, TRAIL = 3, 2


def experts(nc, sem, const, w, x1_d, xt_d, sh_d, y_d):
    ident, eps, mv1 = const["ident"], const["eps"], const["mv_x1"]
    wgt, row_g = const["wgt"], const["row_g"]
    with ExitStack() as ctx:
        def sb(name, shape, dt=F32, where=ctx):
            return where.enter_context(nc.sbuf_tensor(name, shape, dt))

        W1h, W1l = sb("W1h", [P, FC, DT, P], F32R), sb("W1l", [P, FC, DT, P], F32R)
        W2h, W2l = sb("W2h", [P, FC, D], F32R), sb("W2l", [P, FC, D], F32R)
        L1h, L1l = sb("L1h", [P, DT, P], F32R), sb("L1l", [P, DT, P], F32R)
        L2 = sb("L2", [L3, D], F32R)
        X = [(sb(f"X{n}h", [P, DT, r], F32R), sb(f"X{n}l", [P, DT, r], F32R)) for n, r in (("a", 512), ("b", 512))]
        h32 = sb("h32", [P, 512])
        hh = [sb(f"hh{q}", [P, 512], F32R) for q in range(2)]
        hl = [sb(f"hl{q}", [P, 512], F32R) for q in range(2)]
        raw = [sb(f"raw{q}", [P, 512]) for q in range(RING)]
        xrow = [sb(f"xrow{q}", [P, D]) for q in range(2)]
        yst = [sb(f"yst{q}", [P, D]) for q in range(2)]
        b2bc = sb("b2bc", [P, D])
        lg = sb("lg", [P, NT, E])
        b1T = sb("b1T", [P, (E + 1) * FC])
        b1e = sb("b1e", [P, FC])
        graw = sb("graw", [P, DT, E])
        rs1, nm1 = sb("rs1", [P, NT]), sb("nm1", [P, NT])
        slot_tok = sb("slot_tok", [P, E * ST])
        idx = sb("idx", [P, ST], I32)
        rt = ExitStack()
        OH = sb("OH", [P, K, NT, E], F32, rt)
        RA = sb("RA", [P, K, NT, E], F32, rt)
        RB = sb("RB", [P, K, NT, E], F32, rt)
        U, ones = sb("U", [P, P], F32, rt), sb("ones", [P, P], F32, rt)
        m8, r8, w8 = sb("m8", [P, NT], F32, rt), sb("r8", [P, NT], F32, rt), sb("w8", [P, E], F32, rt)
        mx, pos = sb("mx", [P, K, NT], F32, rt), sb("pos", [P, K, NT], F32, rt)
        tok, tok_f = sb("tok", [P, NT], I32, rt), sb("tok_f", [P, NT], F32, rt)
        count_i = RA[:, :, :, :].rearrange("p k t e -> p (k t e)").bitcast(I32)[:, 0:P]
        count_f = U
        late = RB[:, 1, :, :].rearrange("p t e -> p (t e)").bitcast(I32)
        row_i = late[:, 0:K * NT].rearrange("p (k t) -> p k t", k=K)
        hl_i = late[:, K * NT:3 * K * NT].rearrange("p (h k t) -> p h k t", h=2, k=K)
        hl_f = RA[:, :, :, :].rearrange("p k t e -> p (k t e)")[:, 0:2 * K * NT]\
            .rearrange("p (h k t) -> p h k t", h=2, k=K)
        rt.close()
        X.append((sb("Xch", [P, DT, 256], F32R), sb("Xcl", [P, DT, 256], F32R)))
        low1 = [xrow[0][:, k * P:(k + 1) * P] for k in range(HOT)]
        high1 = [xrow[1][:, k * P:k * P + E * ST] for k in range(HOT)]

        psH = [ctx.enter_context(nc.psum_tensor(f"c_psH{q}", [P, 512], F32)) for q in range(2)]
        psT = [ctx.enter_context(nc.psum_tensor(f"c_psT{q}", [P, DT, P], F32)) for q in range(2)]
        psY = [ctx.enter_context(nc.psum_tensor(f"c_psY{t}", [P, D], F32)) for t in range(BT)]

        s_raw = [sem(f"c_raw{q}") for q in range(RING)]
        s_xrow = [sem(f"c_xrow{q}") for q in range(2)]
        s_xg = [sem(f"c_gathered{q}") for q in range(2)]
        s_xts = [sem(f"c_xt_stored{q}") for q in range(2)]
        s_yst = [sem(f"c_y_stored{q}") for q in range(2)]
        s_whi, s_wlo, s_pad, s_gin, s_ghi, s_glo = (
            sem(f"c_{n}") for n in ("weights_hi", "weights_lo", "pad", "gate_in", "gate_hi", "gate_lo"))
        s_bin, s_bt, s_b1, s_b2, s_sd, s_rs, s_nm = (
            sem(f"c_{n}") for n in ("b1_in", "b1_turned", "b1", "b2", "std", "rstd", "nmr"))
        s_norm, s_T, s_xhi, s_xlo = (sem(f"c_{n}") for n in ("normed", "turned", "x_hi", "x_lo"))
        s_mm1, s_gelu, s_hhi, s_hlo, s_mm2, s_yev = (
            sem(f"c_{n}") for n in ("hidden", "gelu", "h_hi", "h_lo", "mm2", "y_out"))
        s_lT, s_lP, s_lg = (sem(f"c_{n}") for n in ("logits_T", "logits_turned", "logits"))
        s_rc, s_v, s_ex, s_cum, s_rows, s_low, s_high, s_add, s_idx = (
            sem(f"c_{n}") for n in ("router_consts", "router_step", "router_exp", "cumulated",
                                    "rows", "low_one_hot", "high_one_hot", "slots_added", "expert_slots"))
        s_cf, s_st = sem("c_counts"), sem("c_slot_tokens")
        s_b1e = sem("c_b1_expert")
        g_sp, g_pool, g_pe, g_act, g_dve = (sem(f"c_gate_{n}") for n in ("sp", "pool", "pe", "act", "dve"))
        block = ctx.enter_context(nc.Block("experts"))

        def shared(b):
            return dict(B=b, t0=b * BT, th=b * (BT // 2), n=BT, gathered=False)

        def expert(e, k):
            o, n = EB[k]
            return dict(B=e * 3 + SB + k, t0=e * ST + NT + o, th=e * (ST // 2) + (NT + o) // 2, n=n,
                        gathered=True)

        X_OF = (2, 0, 1)

        def piece(wset, w_):
            W1, W2, WD, WU = wset
            r = raw[w_ % RING]
            if w_ < 2:
                a = slice(2 * w_, 2 * w_ + 2)
                v = r[:, 0:2 * LR].rearrange("p (a n) -> p a n", a=2)
                hi, lo = (m[:, a, 0:L3].rearrange("p a (g n) -> p a g n", g=3) for m in (L1h, L1l))
                return (WD.rearrange("(a p) n -> p a n", p=P)[:, a, :], v, hi, lo,
                        v.unsqueeze(2).to_broadcast([P, 2, 3, LR]))
            if w_ < 4:
                a = slice((w_ - 2) * 256, (w_ - 1) * 256)
                return WU[:, a], r[0:L3, 0:256], L2[:, a], L2[0:LR, a], r[0:L3, 0:256]
            j = (w_ - 4) // 2
            if w_ % 2 == 0:
                v = r[:, :].rearrange("p (a n) -> p a n", a=DT)
                return (W1.rearrange("(a p) f -> p a f", p=P)[:, :, j * P:(j + 1) * P], v,
                        W1h[:, j, :, :], W1l[:, j, :, :], v)
            return W2[j * P:(j + 1) * P, :], r[:, :], W2h[:, j, :], W2l[:, j, :], r[:, :]

        def pieces_of(j):
            return range(0, 4) if j == 0 else range(2 + 2 * j, 4 + 2 * j)

        def weights_of(e):
            def at(a):
                return a[bass.ds(e, 1), :, :].rearrange("o r c -> (o r) c")
            return at(w["w1"]), at(w["w2"]), at(w["wd"]), at(w["wu"])

        SHARED_W = (w["sw1"], w["sw2"], w["swd"], w["swu"])
        y_v = y_d.rearrange("(e j p) d -> e p j d", e=E, j=ST)

        @block.sync
        def _(sp):
            def load_chunk(s, wset, j):
                for w_ in pieces_of(j):
                    pass_gate(sp, s_wlo, s * PIECES + w_ - RING + 1, g_sp)
                    src, view = piece(wset, w_)[:2]
                    if w_ in (2, 3):
                        for g in range(2):
                            sp.dma_start(view[g * LR:(g + 1) * LR, :], src).then_inc(s_raw[w_ % RING], 16)
                        view = view[2 * LR:L3, :]
                    sp.dma_start(view, src).then_inc(s_raw[w_ % RING], 16)

            def load_pieces(s, wset):
                for j in range(J):
                    load_chunk(s, wset, j)

            def row_in(b, t):
                at, q = shared(b), t % 2
                pass_gate(sp, s_T, at["t0"] + t - 1, g_sp)
                pass_gate(sp, s_xts[q], (at["th"] + t // 2) * 16, g_sp)
                sp.dma_start(xrow[q][:, :], x1_d[bass.ds(b * (BT * P) + t * P, P), :]).then_inc(s_xrow[q], 16)

            def row_out(b, t):
                q = t % 2
                pass_gate(sp, s_norm, b * BT + t + 1, g_sp)
                sp.dma_start(xt_d[bass.ds(b * (BT * P) + t * P, P), :], xrow[q][:, :]).then_inc(s_xts[q], 16)

            def rows(b):
                for t in range(BT):
                    row_in(b, t)
                    row_out(b, t)

            def store(at, dest):
                for t in range(at["n"]):
                    pass_gate(sp, s_yev, at["t0"] + t + 1, g_sp)
                    sp.dma_start(dest(t), yst[t % 2][:, :]).then_inc(s_yst[t % 2], 16)

            def store_shared(b):
                store(shared(b), lambda t: sh_d[bass.ds(b * (BT * P) + t * P, P), :])

            def store_expert(e, k):
                store(expert(e, k), lambda t: y_v[bass.ds(e, 1), :, EB[k][0] + t, :].rearrange("o p d -> (o p) d"))

            def bias2(e, at):
                pass_gate(sp, s_yev, at["t0"], g_sp)
                sp.dma_start(b2bc[:, :], w["b2"][bass.ds(e, 1), :].rearrange("o d -> (o d)").partition_broadcast(P))\
                    .then_inc(s_b2, 16)

            sp.dma_start(raw[0][:, 0:P], w["b1"].rearrange("e (c p) -> (e c) p", p=P)).then_inc(s_bin, 16)
            sp.dma_start(raw[1][0:FC, 0:P], w["sb1"].rearrange("(c p) -> c p", p=P)).then_inc(s_bin, 16)
            sp.dma_start(b2bc[:, :], w["sb2"].partition_broadcast(P)).then_inc(s_b2, 16)
            sp.dma_start(graw[:, :, :], w["gate"].rearrange("(a p) e -> p a e", p=P)).then_inc(s_gin, 16)
            rows(0)
            sp.wait_ge(s_bt, 2)
            for j in range(J):
                load_chunk(0, SHARED_W, j)
                if j - 2 in FRONT:
                    row_in(1, FRONT.index(j - 2))
                if j - 4 in FRONT:
                    row_out(1, FRONT.index(j - 4))
            row_out(1, BT - 1)
            with sp.Fori(1, SB - 1) as b:
                store_shared(b - 1)
                rows(b + 1)
            store_shared(SB - 2)
            load_pieces(1, weights_of(0))
            store_shared(SB - 1)
            bias2(0, expert(0, 0))
            store_expert(0, 0)
            store_expert(0, 1)

            def steady(e):
                load_pieces(e + 1, weights_of(e))
                store_expert(e - 1, 2)
                bias2(e, expert(e, 0))
                store_expert(e, 0)
                store_expert(e, 1)

            with sp.Fori(1, E) as e:
                steady(e)
            store_expert(E - 1, 2)
            for q in range(2):
                sp.wait_ge(s_yst[q], (NT + E * ST) // 2 * 16)
                sp.wait_ge(s_xts[q], NT // 2 * 16)

        @block.scalar
        def _(act):
            def convert(s, w_, used=None):
                _, _, hi, _, view = piece(SHARED_W, w_)
                act.wait_ge(s_raw[w_ % RING], (s * (PIECES // RING) + w_ // RING + 1 + (2 * s + 2) * (w_ % RING > 1)) * 16)
                if used is not None:
                    act.wait_ge(s_mm2, used)
                nc.scalar.copy(hi, view).then_inc(s_whi, 1)

            def convert_chunk(s, j, old=None):
                for w_ in pieces_of(j):
                    convert(s, w_, None if old is None else old["B"] * J + j + 1)

            def normalise(b, t):
                at = shared(b)
                pass_gate(act, s_xrow[t % 2], (at["th"] + t // 2 + 1) * 16, g_act)
                col = b * BT + t
                nc.scalar.activation(xrow[t % 2][:, :], xrow[t % 2][:, :], ACT.Identity,
                                     bias=nm1[:, bass.ds(col, 1)], scale=rs1[:, bass.ds(col, 1)]).then_inc(s_norm, 1)

            def x_hi(at, xb, used, t):
                act.wait_ge(s_T, at["t0"] + t + 1)
                if used is not None:
                    after(act, s_mm1, used)
                nc.scalar.copy(X[xb][0][:, :, t * P:(t + 1) * P], psT[t % 2][:, :, :]).then_inc(s_xhi, 1)

            def run(at, b1, logits=False, nxt=None, wset=None, lead=False, extra=None):
                G, n = at["B"] * J, at["n"]
                for j in range(J):
                    if lead and j + LEAD < J:
                        convert_chunk(0, j + LEAD)
                    if nxt and nxt[3] and j + 1 in FRONT:
                        nxt[3](FRONT.index(j + 1))
                    act.wait_ge(s_mm1, G + j + 1)
                    after(act, s_hlo, G + j)
                    if j == 0:
                        nc.scalar.activation(h32[0:L3, 0:n * P], psH[0][0:L3, 0:n * P], ACT.Gelu).then_inc(s_gelu, 1)
                        if logits:
                            nc.scalar.copy(h32[L3:L3 + E, :], psH[0][L3:L3 + E, :]).then_inc(s_lT, 1)
                    else:
                        if logits and j == 1:
                            act.wait_ge(s_lP, at["B"] + 1)
                        nc.scalar.activation(h32[:, 0:n * P], psH[j % 2][:, 0:n * P], ACT.Gelu,
                                             bias=b1[:, j - 1:j]).then_inc(s_gelu, 1)
                    if nxt and j - 1 in FRONT and FRONT.index(j - 1) < nxt[0]["n"]:
                        x_hi(*nxt[:3], FRONT.index(j - 1))
                    if extra and j in extra:
                        extra[j]()
                    if wset is not None and j >= TRAIL:
                        convert_chunk(wset, j - TRAIL, at)
                if wset is not None:
                    for j in range(J - TRAIL, J):
                        convert_chunk(wset, j, at)

            nc.scalar.activation(rs1[:, :], mv1[:, :, 1], ACT.Sqrt, bias=eps[:, :]).then_inc(s_sd, 1)
            act.wait_ge(s_pad, 2)
            act.wait_ge(s_gin, 16)
            nc.scalar.copy(L1h[:, :, L3:L3 + E], graw[:, :, :]).then_inc(s_ghi, 1)
            act.wait_ge(s_nm, 1)
            for t in range(BT):
                normalise(0, t)
                x_hi(shared(0), 0, None, t)
            act.wait_ge(s_bt, 1)
            nc.scalar.copy(b1T[:, 0:E * FC], psH[0][:, 0:E * FC]).then_inc(s_b1, 1)
            act.wait_ge(s_bt, 2)
            nc.scalar.copy(b1T[:, E * FC:], psH[1][:, 0:FC]).then_inc(s_b1, 1)
            act.wait_ge(s_b1, 2)
            for j in range(LEAD):
                convert_chunk(0, j)

            def shared_block(b, q, **more):
                run(shared(b), b1T[:, E * FC:], logits=True,
                    nxt=(shared(b + 1), 1 - q, b * J, lambda t: normalise(b + 1, t)), **more)

            shared_block(0, 0, lead=True)
            with act.Fori(0, SB // 2 - 1) as i:
                shared_block(i * 2 + 1, 1)
                shared_block(i * 2 + 2, 0)
            def exponentials():
                act.wait_ge(s_v, 2)
                nc.scalar.activation(lg[:, :, :], lg[:, :, :], ACT.Exp).then_inc(s_ex, 1)

            run(shared(SB - 1), b1T[:, E * FC:], logits=True, wset=1, extra={2: exponentials})
            for t in range(EB[0][1]):
                x_hi(expert(0, 0), X_OF[0], None, t)

            def expert_blocks(e, last=False):
                def nxt(e_, k):
                    return (expert(e_, k), X_OF[k], (expert(e_, k)["B"] - 2) * J, None)
                pass_gate(act, s_gelu, expert(e, 0)["B"] * J, g_act)
                nc.scalar.copy(b1e[:, :], b1T[:, bass.ds(e * FC, FC)]).then_inc(s_b1e, 1)
                act.wait_ge(s_b1e, e + 1)
                run(expert(e, 0), b1e, nxt=nxt(e, 1))
                run(expert(e, 1), b1e, nxt=nxt(e, 2))
                if last:
                    run(expert(e, 2), b1e)
                else:
                    run(expert(e, 2), b1e, nxt=nxt(e + 1, 0), wset=e + 2)

            with act.Fori(0, E - 1) as e:
                expert_blocks(e)
            expert_blocks(E - 1, last=True)

        @block.gpsimd
        def _(pool):
            def lows(s, j):
                for w_ in pieces_of(j):
                    _, _, hi, lo, view = piece(SHARED_W, w_)
                    if w_ in (2, 3):
                        hi, view = lo, view[0:LR, :]
                    pool.wait_ge(s_whi, s * PIECES + w_ + 1)
                    nc.gpsimd.tensor_tensor(lo, view, hi.bitcast(F32), ALU.subtract).then_inc(s_wlo, 1)

            def gather(e, k, t):
                at = expert(e, k)
                pass_gate(pool, s_T, at["t0"] + t - 1, g_pool)
                nc.gpsimd.indirect_dma_start(
                    out=xrow[t % 2][:, :], out_offset=None, in_=xt_d[:, :],
                    in_offset=bass.IndirectOffsetOnAxis(ap=idx[:, EB[k][0] + t:EB[k][0] + t + 1], axis=0),
                    bounds_check=T - 1).then_inc(s_xg[t % 2], 16)

            def slots(e):
                pass_gate(pool, s_idx, e + 1, g_pool)

            nc.gpsimd.memzero(L1h[:, :, :]).then_inc(s_pad, 1)
            nc.gpsimd.memzero(L1l[:, :, :]).then_inc(s_pad, 1)
            nc.gpsimd.memset(U[:, :], 1.0).then_inc(s_rc, 1)
            nc.gpsimd.memset(ones[:, :], 1.0).then_inc(s_rc, 1)
            nc.gpsimd.iota(tok[:, :], [[P, NT]], base=0, channel_multiplier=1).then_inc(s_rc, 1)
            nc.gpsimd.iota(count_i, [[1, P]], base=0, channel_multiplier=0).then_inc(s_rc, 1)
            for e in range(E):
                nc.gpsimd.memset(w8[:, e:e + 1], float(E - e)).then_inc(s_rc, 1)
            pool.wait_ge(s_rc, 4 + E)
            nc.gpsimd.affine_select(out=U[:, :], in_=U[:, :], compare_op=ALU.is_gt, fill=0.0,
                                    base=0, pattern=[[1, P]], channel_multiplier=-1).then_inc(s_rc, 1)
            pool.wait_ge(s_ghi, 1)
            nc.gpsimd.tensor_tensor(L1l[:, :, L3:L3 + E], graw[:, :, :], L1h[:, :, L3:L3 + E].bitcast(F32),
                                    ALU.subtract).then_inc(s_glo, 1)
            for j in range(J):
                lows(0, j)
            for j in range(J):
                lows(1, j)
            for q in range(2):
                pool.wait_ge(s_xts[q], NT // 2 * 16)
            slots(0)
            for t in range(EB[0][1]):
                gather(0, 0, t)

            def steady(e, last=False):
                for k in (1, 2):
                    for t in range(EB[k][1]):
                        gather(e, k, t)
                if last:
                    return
                slots(e + 1)
                for t in range(EB[0][1]):
                    gather(e + 1, 0, t)
                for j in range(J):
                    lows(e + 2, j)

            with pool.Fori(0, E - 1) as e:
                steady(e)
            steady(E - 1, last=True)

        @block.vector
        def _(dve):
            def x_lo(at, xb, t):
                dve.wait_ge(s_xhi, at["t0"] + t + 1)
                cols = slice(t * P, (t + 1) * P)
                nc.vector.tensor_tensor(X[xb][1][:, :, cols], psT[t % 2][:, :, :], X[xb][0][:, :, cols].bitcast(F32),
                                        ALU.subtract).then_inc(s_xlo, 1)

            def run(at, bias_count, logits=False, nxt=None, extra=None):
                G, n = at["B"] * J, at["n"]
                for j in range(J):
                    a = (slice(0, P), slice(0, n * P))
                    after(dve, s_mm2, G + j - 1 if j >= 2 else G)
                    dve.wait_ge(s_gelu, G + j + 1)
                    if j == 0:
                        two, third = ((slice(*r), a[1]) for r in ((0, 2 * LR), (2 * LR, L3)))
                        nc.vector.tensor_copy(hh[0][two], h32[two])
                        nc.vector.tensor_copy(hl[0][third], h32[third]).then_inc(s_hhi, 1)
                        dve.wait_ge(s_hhi, G + 1)
                        nc.vector.tensor_tensor(hh[0][third], h32[third], hl[0][third].bitcast(F32), ALU.subtract)\
                            .then_inc(s_hlo, 1)
                    else:
                        nc.vector.tensor_copy(hh[j % 2][a], h32[a]).then_inc(s_hhi, 1)
                        dve.wait_ge(s_hhi, G + j + 1)
                        nc.vector.tensor_tensor(hl[j % 2][a], h32[a], hh[j % 2][a].bitcast(F32), ALU.subtract)\
                            .then_inc(s_hlo, 1)
                    if logits and j == 0:
                        dve.wait_ge(s_lP, at["B"] + 1)
                        nc.vector.tensor_copy(lg[:, bass.ds(at["B"] * BT, BT), :],
                                              psH[0][:, 0:BT * E].rearrange("p (t e) -> p t e", e=E)).then_inc(s_lg, 1)
                    if nxt and j - 1 in FRONT and FRONT.index(j - 1) < nxt[0]["n"]:
                        x_lo(*nxt, FRONT.index(j - 1))
                    if extra and j in extra:
                        for part in extra[j]:
                            part()
                dve.wait_ge(s_mm2, G + J)
                dve.wait_ge(s_b2, bias_count)
                for t in range(n):
                    after(dve, s_yst[t % 2], (at["th"] + t // 2) * 16)
                    nc.vector.tensor_tensor(yst[t % 2][:, :], psY[t][:, :], b2bc[:, :], ALU.add).then_inc(s_yev, 1)

            count = [0]

            def step(ins):
                count[0] += 1
                ins.then_inc(s_v, 1)
                dve.wait_ge(s_v, count[0])

            def over_e(a):
                return a.unsqueeze(2).to_broadcast([P, NT, E])

            v = nc.vector
            w8b = w8[:, :].unsqueeze(1).to_broadcast([P, NT, E])

            def less_max():
                dve.wait_ge(s_lg, SB)
                dve.wait_ge(s_rc, 5 + E)
                v.tensor_copy(tok_f[:, :], tok[:, :]).then_inc(s_cf, 1)
                step(v.tensor_reduce(m8[:, :], lg[:, :, :], AXX, ALU.max))
                step(v.tensor_tensor(lg[:, :, :], lg[:, :, :], over_e(m8[:, :]), ALU.subtract))

            def probabilities():
                dve.wait_ge(s_ex, 1)
                step(v.tensor_reduce(m8[:, :], lg[:, :, :], AXX, ALU.add))
                step(v.reciprocal(r8[:, :], m8[:, :]))
                step(v.tensor_tensor(lg[:, :, :], lg[:, :, :], over_e(r8[:, :]), ALU.mult))

            def pick(k):
                step(v.tensor_reduce(wgt[:, k, :], lg[:, :, :], AXX, ALU.max))
                step(v.tensor_tensor(RB[:, k, :, :], lg[:, :, :], over_e(wgt[:, k, :]), ALU.is_equal))
                step(v.tensor_tensor(RB[:, k, :, :], RB[:, k, :, :], w8b, ALU.mult))
                step(v.tensor_reduce(mx[:, k, :], RB[:, k, :, :], AXX, ALU.max))
                step(v.tensor_tensor(OH[:, k, :, :], RB[:, k, :, :], over_e(mx[:, k, :]), ALU.is_equal))
                if k + 1 < K:
                    step(v.scalar_tensor_tensor(lg[:, :, :], OH[:, k, :, :], -2.0, lg[:, :, :], ALU.mult, ALU.add))
                else:
                    assert count[0] == PICKED

            def totals():
                dve.wait_ge(s_cum, 1)
                v.tensor_copy(count_f[:, :], count_i).then_inc(s_cf, 1)
                dve.wait_ge(s_cf, 2)
                step(v.tensor_copy(RB[:, :, :, :].rearrange("p k t e -> p (k t e)"),
                                   psT[1][:, :, :].rearrange("p a b -> p (a b)")))

            def sums(k):
                for e in range(E):
                    step(v.tensor_tensor_scan(RA[:, k, :, e], ones[:, 0:NT], RB[:, k, :, e], 0.0, ALU.mult, ALU.add))

            def places():
                step(v.tensor_tensor(RA[:, :, :, :], RA[:, :, :, :], RB[:, :, :, :], ALU.subtract))
                step(v.tensor_tensor(RA[:, :, :, :].rearrange("p k t e -> p (k t e)"),
                                     RA[:, :, :, :].rearrange("p k t e -> p (k t e)"),
                                     psT[0][:, :, :].rearrange("p a b -> p (a b)"), ALU.add))
                step(v.tensor_tensor(RA[:, :, :, :], RA[:, :, :, :], OH[:, :, :, :], ALU.mult))
                step(v.tensor_reduce(pos[:, :, :].rearrange("p k t -> p (k t)"),
                                     RA[:, :, :, :].rearrange("p k t e -> p (k t) e"), AXX, ALU.add))

            def table_rows():
                keep, row, far = (RB[:, 0, i * 8:(i + 1) * 8, :].rearrange("p (k a) e -> p k (a e)", k=K)
                                  for i in range(3))
                step(v.tensor_scalar(keep, pos[:, :, :], float(CAP), None, ALU.is_lt))
                step(v.tensor_tensor(wgt[:, :, :], wgt[:, :, :], keep, ALU.mult))
                for k in range(K):
                    step(v.tensor_scalar(row[:, k, :], mx[:, k, :], -float(SLOTS), float(E * SLOTS + k * CAP),
                                         ALU.mult, ALU.add))
                step(v.tensor_tensor(row, row, pos[:, :, :], ALU.add))
                step(v.tensor_tensor(far, row, keep, ALU.mult))
                step(v.tensor_copy(row_g[:, :, :], far))
                step(v.tensor_scalar(far, keep, -float(E * SLOTS), float(E * SLOTS), ALU.mult, ALU.add))
                step(v.tensor_tensor(far, far, row, ALU.add))
                step(v.tensor_copy(row_i, far))
                step(v.tensor_scalar(hl_i[:, 0, :, :], row_i, P.bit_length() - 1, None,
                                     ALU.logical_shift_right))
                step(v.tensor_scalar(hl_i[:, 1, :, :], row_i, P - 1, None, ALU.bitwise_and))
                v.tensor_copy(hl_f[:, :, :, :], hl_i[:, :, :, :]).then_inc(s_rows, 1)

            def expert_slots(e):
                pass_gate(dve, s_T, expert(e, 0)["t0"], g_dve)
                v.tensor_copy(idx[:, :], slot_tok[:, bass.ds(e * ST, ST)]).then_inc(s_idx, 1)

            def find_slots():
                dve.wait_ge(s_rows, 1)
                for g in range(K * NT):
                    k, t = g // NT, g % NT
                    after(dve, s_add, g - HOT + 1)
                    v.tensor_scalar(low1[g % HOT], count_f[:, :], hl_f[:, 1, k, t:t + 1], None, ALU.is_equal)\
                        .then_inc(s_low, 1)
                    v.tensor_scalar(high1[g % HOT], count_f[:, 0:E * ST], hl_f[:, 0, k, t:t + 1], tok_f[:, t:t + 1],
                                    ALU.is_equal, ALU.mult).then_inc(s_high, 1)
                dve.wait_ge(s_add, K * NT)
                v.tensor_copy(slot_tok[:, :], psT[0][:, 0, 0:E * ST]).then_inc(s_st, 1)
                dve.wait_ge(s_st, 1)
                expert_slots(0)

            dve.wait_ge(s_sd, 1)
            nc.vector.reciprocal(rs1[:, :], rs1[:, :]).then_inc(s_rs, 1)
            dve.wait_ge(s_rs, 1)
            nc.vector.scalar_tensor_tensor(nm1[:, :], mv1[:, :, 0], -1.0, rs1[:, :], ALU.mult, ALU.mult)\
                .then_inc(s_nm, 1)
            for t in range(BT):
                x_lo(shared(0), 0, t)

            def shared_block(b, q):
                run(shared(b), 16, logits=True, nxt=(shared(b + 1), 1 - q))

            shared_block(0, 0)
            with dve.Fori(0, SB // 2 - 1) as i:
                shared_block(i * 2 + 1, 1)
                shared_block(i * 2 + 2, 0)
            run(shared(SB - 1), 16, logits=True, extra={
                1: (less_max,), 4: (probabilities,), 5: (lambda: pick(0),), 6: (lambda: pick(1),),
                9: (totals, lambda: sums(0)), 10: (lambda: sums(1),), 11: (places,), 12: (table_rows,)})
            find_slots()
            for t in range(EB[0][1]):
                x_lo(expert(0, 0), X_OF[0], t)

            def expert_blocks(e, last=False):
                run(expert(e, 0), (e + 2) * 16, nxt=(expert(e, 1), X_OF[1]))
                run(expert(e, 1), (e + 2) * 16, nxt=(expert(e, 2), X_OF[2]))
                if not last:
                    expert_slots(e + 1)
                run(expert(e, 2), (e + 2) * 16, nxt=None if last else (expert(e + 1, 0), X_OF[0]))

            with dve.Fori(0, E - 1) as e:
                expert_blocks(e)
            expert_blocks(E - 1, last=True)

        @block.tensor
        def _(pe):
            def turn(at, t):
                if at["gathered"]:
                    pe.wait_ge(s_xg[t % 2], (at["th"] - NT // 2 + t // 2 + 1) * 16)
                else:
                    pe.wait_ge(s_norm, at["t0"] + t + 1)
                after(pe, s_xlo, at["t0"] + t - 1)
                for d in range(DT):
                    last = nc.tensor.transpose(psT[t % 2][:, d, :], xrow[t % 2][:, d * P:(d + 1) * P], ident[:, :])
                last.then_inc(s_T, 1)

            def products(out, pairs):
                n = 3 * len(pairs)
                i = 0
                for (ah, al), (bh, bl) in pairs:
                    for a, b in ((ah, bh), (ah, bl), (al, bh)):
                        last = nc.tensor.matmul(out, a, b, start=(i == 0), stop=(i == n - 1))
                        i += 1
                return last

            def run(at, xb, s, logits=False, nxt=None, extra=None):
                G, n = at["B"] * J, at["n"]
                Xh, Xl = X[xb]
                cols = slice(0, n * P)

                def up(j):
                    pe.wait_ge(s_wlo, s * PIECES + (4 if j == 0 else 4 + 2 * j))
                    after(pe, s_gelu, G + j - 1 if j >= 2 else G)
                    if j == 0:
                        pe.wait_ge(s_xlo, at["t0"] + n)
                        wh, wl = L1h, L1l
                        if logits:
                            pe.wait_ge(s_glo, 1)
                    else:
                        wh, wl = W1h[:, j - 1, :, :], W1l[:, j - 1, :, :]
                    if logits and j == 2:
                        pe.wait_ge(s_lg, at["B"] + 1)
                    products(psH[j % 2][:, cols], [((wh[:, d, :], wl[:, d, :]), (Xh[:, d, cols], Xl[:, d, cols]))
                                                   for d in range(DT)]).then_inc(s_mm1, 1)

                def down(j):
                    if j == 0:
                        after(pe, s_yev, at["t0"])
                    pe.wait_ge(s_hlo, G + j + 1)
                    for t in range(n):
                        c = slice(t * P, (t + 1) * P)
                        if j == 0:
                            last = nc.tensor.matmul(psY[t][:, :], hh[0][0:L3, c], L2[:, :], start=True, stop=False)
                            continue
                        wh, wl = W2h[:, j - 1, :], W2l[:, j - 1, :]
                        for i, (a, b) in enumerate(((hh, wh), (hh, wl), (hl, wh))):
                            last = nc.tensor.matmul(psY[t][:, :], a[j % 2][:, c], b,
                                                    start=False, stop=(j == J - 1 and i == 2))
                    last.then_inc(s_mm2, 1)

                up(0)
                for j in range(J):
                    if j + 1 < J:
                        up(j + 1)
                    if logits and j == 0:
                        pass_gate(pe, s_lT, at["B"] + 1, g_pe)
                        for t in range(BT):
                            last = nc.tensor.transpose(psH[0][:, t * E:(t + 1) * E],
                                                       h32[L3:L3 + E, t * P:(t + 1) * P], ident[L3:L3 + E, L3:L3 + E])
                        last.then_inc(s_lP, 1)
                    if nxt and j in FRONT and FRONT.index(j) < nxt["n"]:
                        t = FRONT.index(j)
                        turn(nxt, t)
                    if extra and j in extra:
                        extra[j]()
                    down(j)

            for t in range(BT):
                turn(shared(0), t)
            pe.wait_ge(s_bin, 32)
            nc.tensor.transpose(psH[0][:, 0:P], raw[0][:, 0:P], ident[:, :]).then_inc(s_bt, 1)
            nc.tensor.transpose(psH[1][:, 0:FC], raw[1][0:FC, 0:P], ident[0:FC, 0:FC]).then_inc(s_bt, 1)
            pe.wait_ge(s_b1, 2)

            def shared_block(b, q):
                run(shared(b), q, 0, logits=True, nxt=shared(b + 1))

            shared_block(0, 0)
            with pe.Fori(0, SB // 2 - 1) as i:
                shared_block(i * 2 + 1, 1)
                shared_block(i * 2 + 2, 0)
            def cumulate():
                pe.wait_ge(s_v, PICKED)
                pe.wait_ge(s_rc, 5 + E)
                flat = OH[:, :, :, :].rearrange("p k t e -> p (k t e)")
                nc.tensor.matmul(psT[0][:, :, :].rearrange("p a b -> p (a b)"), U[:, :], flat, start=True, stop=True)
                nc.tensor.matmul(psT[1][:, :, :].rearrange("p a b -> p (a b)"), ones[:, :], flat,
                                 start=True, stop=True).then_inc(s_cum, 1)

            run(shared(SB - 1), 1, 0, logits=True, extra={8: cumulate})
            for g in range(K * NT):
                pe.wait_ge(s_low, g + 1)
                pe.wait_ge(s_high, g + 1)
                nc.tensor.matmul(psT[0][:, 0, 0:E * ST], low1[g % HOT], high1[g % HOT],
                                 start=(g == 0), stop=(g == K * NT - 1)).then_inc(s_add, 1)
            for t in range(EB[0][1]):
                turn(expert(0, 0), t)

            def expert_blocks(e, last=False):
                run(expert(e, 0), X_OF[0], e + 1, nxt=expert(e, 1))
                run(expert(e, 1), X_OF[1], e + 1, nxt=expert(e, 2))
                run(expert(e, 2), X_OF[2], e + 1, nxt=None if last else expert(e + 1, 0))

            with pe.Fori(0, E - 1) as e:
                expert_blocks(e)
            expert_blocks(E - 1, last=True)


def combine(nc, sem, const, x1_d, sh_d, y_d, out):
    wgt, row_g, eps = const["wgt"], const["row_g"], const["eps"]
    N, G = 6, 2
    NG = NT // G
    with ExitStack() as ctx:
        def ring(name, *shape):
            return [ctx.enter_context(nc.sbuf_tensor(f"d_{name}{q}", [P, G, *shape], F32)) for q in range(N)]

        y0, y1, shr, x1r = ring("y0", D), ring("y1", D), ring("sh", D), ring("x1", D)
        st, mv, sd, rs, nm = ring("st", 6), ring("mv", 2), ring("sd"), ring("rs"), ring("nm")
        s_g0, s_g1, s_l, s_o = ([sem(f"d_{n}{q}") for q in range(N)]
                                for n in ("first_gathered", "second_gathered", "loaded", "stored"))
        s_a, s_b, s_c, s_st, s_mv, s_sd, s_rs, s_nm, s_n, s_x = (
            sem(f"d_{n}") for n in ("w0y0", "w1y1", "sum", "stats", "meanvar", "std", "rstd", "nmr", "normed", "x2"))
        block = ctx.enter_context(nc.Block("combine"))

        @block.sync
        def _(sp):
            def rows(a, g):
                return a[g * G * P:(g + 1) * G * P, :].rearrange("(t p) d -> p t d", p=P)

            def store(g):
                sp.wait_ge(s_x, (g + 1) * G)
                sp.dma_start(rows(out, g), y0[g % N][:, :, :]).then_inc(s_o[g % N], 16)

            for g in range(NG):
                q = g % N
                after(sp, s_x, (g - N + 1) * G)
                sp.dma_start(shr[q][:, :, :], rows(sh_d, g)).then_inc(s_l[q], 16)
                sp.dma_start(x1r[q][:, :, :], rows(x1_d, g)).then_inc(s_l[q], 16)
                if g >= N - 2:
                    store(g - N + 2)
            for g in range(NG - N + 2, NG):
                store(g)
            for q in range(N):
                sp.wait_ge(s_o[q], len(range(q, NG, N)) * 16)

        @block.gpsimd
        def _(pool):
            for g in range(NG):
                q = g % N
                after(pool, s_o[q], g // N * 16)
                for k, (dst, s_g) in enumerate(((y0, s_g0), (y1, s_g1))):
                    for t in range(G):
                        nc.gpsimd.indirect_dma_start(
                            out=dst[q][:, t, :], out_offset=None, in_=y_d[:, :],
                            in_offset=bass.IndirectOffsetOnAxis(ap=row_g[:, k, g * G + t:g * G + t + 1], axis=0),
                            bounds_check=E * SLOTS - 1).then_inc(s_g[q], 16)

        @block.scalar
        def _(act):
            def weigh(g):
                q = g % N
                act.wait_ge(s_g0[q], (g // N + 1) * G * 16)
                for t in range(G):
                    nc.scalar.mul(y0[q][:, t, :], y0[q][:, t, :], wgt[:, 0, g * G + t:g * G + t + 1]).then_inc(s_a, 1)

            def norm(g):
                q = g % N
                act.wait_ge(s_mv, (g + 1) * G)
                nc.scalar.activation(sd[q][:, :], mv[q][:, :, 1], ACT.Sqrt, bias=eps[:, :]).then_inc(s_sd, 1)
                act.wait_ge(s_nm, g + 1)
                for t in range(G):
                    nc.scalar.activation(y0[q][:, t, :], y0[q][:, t, :], ACT.Identity, bias=nm[q][:, t:t + 1],
                                         scale=rs[q][:, t:t + 1]).then_inc(s_n, 1)

            for g in range(NG):
                weigh(g)
                if g >= 1:
                    norm(g - 1)
            norm(NG - 1)

        @block.vector
        def _(dve):
            v = nc.vector

            def add(g):
                q = g % N
                dve.wait_ge(s_g1[q], (g // N + 1) * G * 16)
                for t in range(G):
                    dve.wait_ge(s_a, g * G + t + 1)
                    v.scalar_tensor_tensor(y0[q][:, t, :], y1[q][:, t, :], wgt[:, 1, g * G + t:g * G + t + 1],
                                           y0[q][:, t, :], ALU.mult, ALU.add).then_inc(s_b, 1)
                dve.wait_ge(s_l[q], (g // N + 1) * 32)
                for t in range(G):
                    dve.wait_ge(s_b, g * G + t + 1)
                    v.scalar_tensor_tensor(y0[q][:, t, :], shr[q][:, t, :], 0.2, y0[q][:, t, :], ALU.mult, ALU.add)\
                        .then_inc(s_c, 1)
                for t in range(G):
                    dve.wait_ge(s_c, g * G + t + 1)
                    v.bn_stats(st[q][:, t, :], y0[q][:, t, :]).then_inc(s_st, 1)
                for t in range(G):
                    dve.wait_ge(s_st, g * G + t + 1)
                    v.bn_aggr(mv[q][:, t, :], st[q][:, t, :]).then_inc(s_mv, 1)

            def scale(g):
                q = g % N
                dve.wait_ge(s_sd, g + 1)
                v.reciprocal(rs[q][:, :], sd[q][:, :]).then_inc(s_rs, 1)
                dve.wait_ge(s_rs, g + 1)
                v.scalar_tensor_tensor(nm[q][:, :], mv[q][:, :, 0], -1.0, rs[q][:, :], ALU.mult, ALU.mult)\
                    .then_inc(s_nm, 1)

            def residual(g):
                q = g % N
                for t in range(G):
                    dve.wait_ge(s_n, g * G + t + 1)
                    v.tensor_tensor(y0[q][:, t, :], y0[q][:, t, :], x1r[q][:, t, :], ALU.add).then_inc(s_x, 1)

            for g in range(NG):
                add(g)
                if g >= 1:
                    scale(g - 1)
                if g >= 2:
                    residual(g - 2)
            scale(NG - 1)
            residual(NG - 2)
            residual(NG - 1)


_INS = dict(x="L0_attn_x", A_log="L0_attn_A_log", D_skip="L0_attn_D_skip", W_x="L0_attn_W_x", W_dt="L0_attn_W_dt",
            b_dt="L0_attn_b_dt", gate="L0_ffn_gate_w", w1="L0_ffn_w1", b1="L0_ffn_b1", w2="L0_ffn_w2", b2="L0_ffn_b2",
            wd="L0_ffn_wd", wu="L0_ffn_wu", sw1="L0_ffn_sw1", sb1="L0_ffn_sb1", sw2="L0_ffn_sw2", sb2="L0_ffn_sb2",
            swd="L0_ffn_swd", swu="L0_ffn_swu")


def program(nc, a, out):
    with ExitStack() as ctx:
        def sem(name):
            return ctx.enter_context(nc.semaphore(name))

        def dram(name, shape, dt=F32):
            return nc.dram_tensor(name, shape, dt).ap()

        dt_d, dtx_d = dram("dt_d", (DT, P, T)), dram("dtx_d", (DT, P, T))
        bc_d, skip_d = dram("bc_d", (2 * NS, T)), dram("skip_d", (T, D))
        x1_d, xt_d, sh_d = dram("x1_d", (T, D)), dram("xt_d", (T, D)), dram("sh_d", (T, D))
        y_d = dram("y_d", (E * SLOTS, D))
        const = {n: ctx.enter_context(nc.sbuf_tensor(n, s, d)) for n, s, d in (
            ("ident", [P, P], F32), ("eps", [P, 1], F32), ("mv_x1", [P, NT, 2], F32),
            ("wgt", [P, K, NT], F32), ("row_g", [P, K, NT], I32))}
        with nc.sbuf_tensor("A_neg", [P, DT, NS], F32) as const["A_neg"]:
            prepare(nc, sem, const, a["x"], a["A_log"], a["D_skip"], a["W_x"], a["W_dt"], a["b_dt"],
                    dt_d, dtx_d, bc_d, skip_d)
            scan(nc, sem, const, a["x"], dt_d, dtx_d, bc_d, skip_d, x1_d)
        experts(nc, sem, const, a, x1_d, xt_d, sh_d, y_d)
        combine(nc, sem, const, x1_d, sh_d, y_d, out)


def kernel(**inputs):
    import numpy as np
    import concourse.bacc as bacc
    from concourse.bass_utils import run_bass_kernel_spmd

    nc = bacc.Bacc("TRN2", target_bir_lowering=False, num_devices=1)
    arrays = {short: np.ascontiguousarray(inputs[name]) for short, name in _INS.items()}
    arrays["x"] = arrays["x"].reshape(T, D)
    arrays = {f"in_{short}": v for short, v in arrays.items()}
    aps = {n[3:]: nc.dram_tensor(n, v.shape, F32, kind="ExternalInput").ap() for n, v in arrays.items()}
    out = nc.dram_tensor("out", (T, D), F32, kind="ExternalOutput").ap()
    program(nc, aps, out)
    r = run_bass_kernel_spmd(nc, [arrays], core_ids=[0])
    return r.results[0]["out"].reshape(1, T, D)
```
